# Optimizing a Trainium2 kernel written in Bass

```python
import numpy as np
import jax
import jax.numpy as jnp

def _softmax(x, axis=-1):
    return jax.nn.softmax(x, axis=axis)
def _gelu(x):
    return jax.nn.gelu(x, approximate=True)
def _silu(x):
    return jax.nn.silu(x)
def _sigmoid(x):
    return jax.nn.sigmoid(x)
def _layernorm(x, axis=-1, eps=1e-5):
    m = jnp.mean(x, axis=axis, keepdims=True)
    v = jnp.var(x, axis=axis, keepdims=True)
    return (x - m) / jnp.sqrt(v + eps)
def _scatter_add(tgt, idx, src, axis=0):
    return tgt.at[idx].add(src)
def _segment_sum(src, seg, n):
    return jax.ops.segment_sum(src, seg, n)

kernel_name = 'mk_metaformer_d1_conv_nchw512_0ce8b9'

def setup_inputs(seed: int = 0):
    np.random.seed(seed)
    _w = jnp.asarray
    def _rec_inputs():
        import jax
        import jax.numpy as jnp
        _gk = jax.random.key(seed)
        x = -0.0005207 + 1.001 * jax.random.normal(jax.random.fold_in(_gk, 1), (1, 512, 64, 64), jnp.float32)
        return x
    x = _rec_inputs()
    def _L0_conv_setup():
        import jax, jax.numpy as jnp
        import numpy as np
        B, C, H, W = (1, 512, 64, 64)
        HEADS, DH = (4, 128)
        SCALE = DH ** (-0.5)

        def rel_to_abs(x):
            b, h, l, _ = x.shape
            x = jnp.pad(x, ((0, 0), (0, 0), (0, 0), (0, 1)))
            flat = x.reshape(b, h, l * 2 * l)
            flat = jnp.pad(flat, ((0, 0), (0, 0), (0, l - 1)))
            return flat.reshape(b, h, l + 1, 2 * l - 1)[:, :, :l, l - 1:]

        def relative_logits_1d(q, rel_k):
            b, heads, hh, ww, d = q.shape
            logits = jnp.einsum('bhxyd,rd->bhxyr', q, rel_k)
            logits = logits.reshape(b, heads * hh, ww, 2 * ww - 1)
            logits = rel_to_abs(logits).reshape(b, heads, hh, ww, ww)
            return jnp.broadcast_to(logits[:, :, :, None], (b, heads, hh, hh, ww, ww))

        def rel_pos_bias(q, rel_height, rel_width):
            b = q.shape[0]
            q2 = q.reshape(b, HEADS, H, W, DH)
            lw = relative_logits_1d(q2, rel_width)
            lw = lw.transpose(0, 1, 2, 4, 3, 5).reshape(b, HEADS, H * W, H * W)
            qt = q2.transpose(0, 1, 3, 2, 4)
            lh = relative_logits_1d(qt, rel_height)
            lh = lh.transpose(0, 1, 4, 2, 5, 3).reshape(b, HEADS, H * W, H * W)
            return lw + lh
        key = jax.random.key(seed)
        k1, k2, k3, k4 = jax.random.split(key, 4)
        fmap = jax.random.normal(k1, (B, C, H, W), jnp.float32)
        w_qkv = jax.random.normal(k2, (3 * HEADS * DH, C), jnp.float32) * C ** (-0.5)
        rel_height = jax.random.normal(k3, (2 * H - 1, DH), jnp.float32) * SCALE
        rel_width = jax.random.normal(k4, (2 * W - 1, DH), jnp.float32) * SCALE
        return {'fmap': fmap, 'w_qkv': w_qkv, 'rel_height': rel_height, 'rel_width': rel_width}
    _L0_conv_all = _L0_conv_setup()
    _L0_conv_in = {k: v for k, v in _L0_conv_all.items() if k in ('w_qkv', 'rel_height', 'rel_width', )}
    del _L0_conv_all

    def _L0_ffn_setup():
        import jax, jax.numpy as jnp
        import numpy as np
        BINS = jnp.array([-1.5, -1.0, -0.5, 0.0, 0.5, 1.0, 1.5], dtype=jnp.float32)
        N_BINS = BINS.shape[0] + 1
        INDEX = 0
        key = jax.random.key(seed)
        k1, k2 = jax.random.split(key)
        x = jax.random.normal(k1, (8, 4096, 512), dtype=jnp.float32)
        W = jax.random.normal(k2, (N_BINS, 512, 512), dtype=jnp.float32) * 0.02
        return {'x': x, 'W': W}
    _L0_ffn_all = _L0_ffn_setup()
    _L0_ffn_in = {k: v for k, v in _L0_ffn_all.items() if k in ('W', )}
    del _L0_ffn_all

    return {
        "x": x,
        "L0_conv_w_qkv": _L0_conv_in["w_qkv"],
        "L0_conv_rel_height": _L0_conv_in["rel_height"],
        "L0_conv_rel_width": _L0_conv_in["rel_width"],
        "L0_ffn_W": _L0_ffn_in["W"],
    }

def reference(x, L0_conv_w_qkv, L0_conv_rel_height, L0_conv_rel_width, L0_ffn_W):
    import jax
    import jax.numpy as jnp
    def _L0_conv_ref(fmap, w_qkv, rel_height, rel_width):
        import jax, jax.numpy as jnp
        import numpy as np
        B, C, H, W = (1, 512, 64, 64)
        HEADS, DH = (4, 128)
        SCALE = DH ** (-0.5)

        def rel_to_abs(x):
            b, h, l, _ = x.shape
            x = jnp.pad(x, ((0, 0), (0, 0), (0, 0), (0, 1)))
            flat = x.reshape(b, h, l * 2 * l)
            flat = jnp.pad(flat, ((0, 0), (0, 0), (0, l - 1)))
            return flat.reshape(b, h, l + 1, 2 * l - 1)[:, :, :l, l - 1:]

        def relative_logits_1d(q, rel_k):
            b, heads, hh, ww, d = q.shape
            logits = jnp.einsum('bhxyd,rd->bhxyr', q, rel_k)
            logits = logits.reshape(b, heads * hh, ww, 2 * ww - 1)
            logits = rel_to_abs(logits).reshape(b, heads, hh, ww, ww)
            return jnp.broadcast_to(logits[:, :, :, None], (b, heads, hh, hh, ww, ww))

        def rel_pos_bias(q, rel_height, rel_width):
            b = q.shape[0]
            q2 = q.reshape(b, HEADS, H, W, DH)
            lw = relative_logits_1d(q2, rel_width)
            lw = lw.transpose(0, 1, 2, 4, 3, 5).reshape(b, HEADS, H * W, H * W)
            qt = q2.transpose(0, 1, 3, 2, 4)
            lh = relative_logits_1d(qt, rel_height)
            lh = lh.transpose(0, 1, 4, 2, 5, 3).reshape(b, HEADS, H * W, H * W)
            return lw + lh
        b = fmap.shape[0]
        qkv = jnp.einsum('oc,bchw->bohw', w_qkv, fmap)
        q, k, v = jnp.split(qkv, 3, axis=1)

        def to_heads(t):
            return t.reshape(b, HEADS, DH, H * W).transpose(0, 1, 3, 2)
        q, k, v = map(to_heads, (q, k, v))
        q = q * SCALE
        sim = jnp.einsum('bhid,bhjd->bhij', q, k)
        sim = sim + rel_pos_bias(q, rel_height, rel_width)
        attn = jax.nn.softmax(sim, axis=-1)
        out = jnp.einsum('bhij,bhjd->bhid', attn, v)
        return out.transpose(0, 1, 3, 2).reshape(b, HEADS * DH, H, W)

    def _L0_ffn_ref(x, W):
        import jax, jax.numpy as jnp
        import numpy as np
        BINS = jnp.array([-1.5, -1.0, -0.5, 0.0, 0.5, 1.0, 1.5], dtype=jnp.float32)
        N_BINS = BINS.shape[0] + 1
        INDEX = 0
        y = x[..., INDEX]
        mem = jnp.sum(y[..., None] > BINS, axis=-1)
        B, T, D = x.shape
        xf = x.reshape(B * T, D)
        memf = mem.reshape(B * T)
        out = jnp.zeros((B * T, W.shape[-1]), dtype=x.dtype)
        for k in range(N_BINS):
            sel = (memf == k)[:, None].astype(x.dtype)
            out = out + sel * (xf @ W[k])
        return out.reshape(B, T, W.shape[-1])

    def _gn(v, G=32, eps=1e-5):
        B_, C_, H_, W_ = v.shape
        g = v.reshape(B_, G, C_ // G, H_, W_)
        m = jnp.mean(g, axis=(2, 3, 4), keepdims=True)
        s = jnp.var(g, axis=(2, 3, 4), keepdims=True)
        return ((g - m) / jnp.sqrt(s + eps)).reshape(v.shape)

    def _ln_c(v, eps=1e-6):
        m = jnp.mean(v, axis=1, keepdims=True)
        s = jnp.var(v, axis=1, keepdims=True)
        return (v - m) / jnp.sqrt(s + eps)

    def _ln_t(v, eps=1e-5):
        m = jnp.mean(v, axis=-1, keepdims=True)
        s = jnp.var(v, axis=-1, keepdims=True)
        return (v - m) / jnp.sqrt(s + eps)

    def _to_tokens(v):
        B_, C_, H_, W_ = v.shape
        return v.reshape(B_, C_, H_ * W_).transpose(0, 2, 1)
    def _from_tokens(t, like):
        B_, C_, H_, W_ = like.shape
        return t.transpose(0, 2, 1).reshape(B_, C_, H_, W_)

    x = x + _L0_conv_ref(_ln_c(x), L0_conv_w_qkv, L0_conv_rel_height, L0_conv_rel_width)
    t = _to_tokens(x)
    t = t + _L0_ffn_ref(_ln_t(t), L0_ffn_W)
    x = _from_tokens(t, x)
    return x


_drawn_inputs = setup_inputs


def setup_inputs(seed=0):
    import zlib

    import numpy as np

    out = dict(_drawn_inputs(seed))
    spreads = {}
    factors = {}
    for name, (base, spread) in spreads.items():
        noise = np.random.default_rng([zlib.crc32(name.encode()), seed]).standard_normal(out[name].shape)
        drawn = base * np.exp(spread * noise) if base else spread * noise
        out[name] = jnp.asarray(drawn.astype(out[name].dtype))
    for name, factor in factors.items():
        out[name] = (out[name] * factor).astype(out[name].dtype)
    return out
```

```python
from contextlib import ExitStack

import concourse.bass as bass
from concourse import mybir
from concourse.alu_op_type import AluOpType as ALU

P = 128
C = 512
CC = C // P
SIDE = 64
T = SIDE * SIDE
HEADS = 4
DH = C // HEADS
B = 512
NB = T // B
TPB = B // P
JT = T // P
ROWS = B // SIDE
BINS = 8
THRESHOLDS = [-1.5, -1.0, -0.5, 0.0, 0.5, 1.0, 1.5]
SCALE = DH ** -0.5
EPS_C = 1e-6
EPS_T = 1e-5
WIN = SIDE + ROWS - 1

F32 = mybir.dt.float32
F32R = mybir.dt.float32r
ACT = mybir.ActivationFunctionType
AX = mybir.AxisListType


def f32(ap):
    return ap.bitcast(F32)


def own_wait(eng, passed):
    eng.sem_inc(passed, 1)


def split_product(pe, out, w_hi, w_lo, m_hi, m_lo, first, last):
    pe.matmul(out, w_lo, m_hi, start=first, stop=False)
    pe.matmul(out, w_hi, m_lo, start=False, stop=False)
    return pe.matmul(out, w_hi, m_hi, start=False, stop=last)


def project(nc, sem, x, w_qkv_t, rel_w_t, rel_h_t, q_dram, k_dram, v_dram, rw_dram):
    OUTS = 3 * HEADS
    RING = 4
    PER = OUTS // RING

    with ExitStack() as ctx:
        def sb(name, shape, dt=F32):
            return ctx.enter_context(nc.sbuf_tensor(name, shape, dt))

        def ps(name):
            return ctx.enter_context(nc.psum_tensor(name, [P, B], F32))

        w_raw = sb("p_w_raw", [P, CC, 3 * C])
        w_hi = sb("p_w_hi", [P, CC, 3 * C], F32R)
        w_lo = sb("p_w_lo", [P, CC, 3 * C], F32R)
        rel_w = sb("p_rel_w", [P, P])
        rel_h = sb("p_rel_h", [P, 2, WIN])
        mean_w = sb("p_mean_w", [P, P])
        x_in = [sb(f"p_x{i}", [P, CC, B]) for i in range(2)]
        xc = sb("p_xc", [P, CC, B])
        sq = sb("p_sq", [P, CC, B])
        x_hi = [sb(f"p_xhi{i}", [P, CC, B], F32R) for i in range(2)]
        x_lo = [sb(f"p_xlo{i}", [P, CC, B], F32R) for i in range(2)]
        dev = sb("p_dev", [P, B])
        rstd = sb("p_rstd", [P, B])
        newton = sb("p_newton", [P, B])
        eps = sb("p_eps", [P, 1])
        q_f = [sb(f"p_qf{i}", [P, B]) for i in range(2)]
        outs = [sb(f"p_out{i}", [P, 2, B], F32R) for i in range(RING)]
        rw = [sb(f"p_rw{i}", [P, B]) for i in range(2)]
        lh = [sb(f"p_lh{i}", [SIDE, 2, B], F32R) for i in range(2)]

        bank = [ps(f"p_bank{i}") for i in range(RING)]
        mean_ps = ps("p_mean")
        var_ps = ps("p_var")
        rw_ps = ps("p_rwps")
        lh_ps = ps("p_lhps")

        passed = sem("p_passed")
        w_loaded = sem("p_w_loaded")
        rel_loaded = sem("p_rel_loaded")
        w_hi_done = sem("p_w_hi_done")
        w_lo_done = sem("p_w_lo_done")
        const_done = sem("p_const_done")
        x_loaded = [sem(f"p_x_loaded{i}") for i in range(2)]
        win_loaded = [sem(f"p_win_loaded{i}") for i in range(2)]
        mean_done = sem("p_mean_done")
        xc_done = sem("p_xc_done")
        sq_done = sem("p_sq_done")
        var_done = sem("p_var_done")
        dev_done = sem("p_dev_done")
        norm_step = sem("p_norm_step")
        x_hi_done = sem("p_x_hi_done")
        x_lo_done = sem("p_x_lo_done")
        product_done = sem("p_product_done")
        out_stored = [sem(f"p_out_stored{i}") for i in range(RING)]
        hi_done = sem("p_hi_done")
        lo_done = sem("p_lo_done")
        q_f_done = sem("p_q_f_done")
        rel_done = sem("p_rel_done")
        rw_done = sem("p_rw_done")
        lh_hi_done = sem("p_lh_hi_done")
        lh_lo_done = sem("p_lh_lo_done")
        rw_stored = [sem(f"p_rw_stored{i}") for i in range(2)]
        lh_stored = [sem(f"p_lh_stored{i}") for i in range(2)]

        with nc.Block() as block:

            @block.sync
            def _(sp):
                sp.sem_inc(lo_done, RING)
                sp.sem_inc(rel_done, 2)
                sp.sem_inc(rw_done, 1)
                sp.sem_inc(lh_lo_done, 1)
                for i in range(RING):
                    sp.sem_inc(out_stored[i], 32)
                for i in range(2):
                    sp.sem_inc(rw_stored[i], 16)
                    sp.sem_inc(lh_stored[i], 32)

                def load_x(tb, p):
                    sp.dma_start(x_in[p][:, :, :], x[:, bass.ds(tb * B, B)].rearrange("(c p) t -> p c t", p=P)) \
                      .then_inc(x_loaded[p], 16)

                def load_window(tb, p):
                    sp.dma_start(rel_h[:, p, :], rel_h_t[:, bass.ds((NB - 1 - tb) * ROWS, WIN)]) \
                      .then_inc(win_loaded[p], 16)

                load_x(0, 0)
                for c in range(CC):
                    sp.dma_start(w_raw[:, c, :], w_qkv_t[c * P:(c + 1) * P, :]).then_inc(w_loaded, 16)
                sp.dma_start(rel_w[:, :], rel_w_t).then_inc(rel_loaded, 16)
                load_window(0, 0)
                load_x(1, 1)
                load_window(1, 1)

                def store_out(tb, idx):
                    r = idx % RING
                    sp.wait_ge(lo_done, tb * OUTS + idx + 1 + RING)
                    own_wait(sp, passed)
                    cols = bass.ds(tb * B, B)
                    for half in range(2):
                        src = f32(outs[r][:, half, :])
                        if idx < HEADS:
                            dst = q_dram[idx, :, half, cols]
                        elif idx < 2 * HEADS:
                            dst = k_dram[idx - HEADS, :, half, cols]
                        else:
                            jt = tb * TPB + idx - 2 * HEADS
                            dst = v_dram[:, :, half, bass.ds(jt * DH, DH)].rearrange("h p d -> p h d")
                            src = src.rearrange("p (h d) -> p h d", h=HEADS)
                        sp.dma_start(dst, src).then_inc(out_stored[r], 16)

                def store_rel(tb, h):
                    i = h % 2
                    sp.wait_ge(rw_done, tb * HEADS + h + 1 + 1)
                    own_wait(sp, passed)
                    dst = rw_dram[h, bass.ds(tb * B, B), :].rearrange("(k p) r -> p k r", p=P)
                    sp.dma_start(dst, rw[i][:, :].rearrange("p (k r) -> p k r", k=TPB)).then_inc(rw_stored[i], 16)
                    sp.wait_ge(lh_lo_done, tb * HEADS + h + 1 + 1)
                    own_wait(sp, passed)
                    for half in range(2):
                        sp.dma_start(q_dram[h, half * SIDE:(half + 1) * SIDE, 2, bass.ds(tb * B, B)],
                                     f32(lh[i][:, half, :])).then_inc(lh_stored[i], 16)

                def block_io(tb, p, more):
                    for idx in range(OUTS):
                        store_out(tb, idx)
                        if 1 <= idx <= HEADS:
                            store_rel(tb, idx - 1)
                    if more:
                        sp.wait_ge(xc_done, tb + 1)
                        own_wait(sp, passed)
                        load_x(tb + 2, p)
                        sp.wait_ge(rel_done, (tb + 1) * HEADS + 2)
                        own_wait(sp, passed)
                        load_window(tb + 2, p)

                with sp.Fori(0, NB // 2 - 1) as m:
                    block_io(m * 2, 0, True)
                    block_io(m * 2 + 1, 1, True)
                block_io(NB - 2, 0, False)
                block_io(NB - 1, 1, False)
                for i in range(RING):
                    sp.wait_ge(out_stored[i], 32 * (NB * PER + 1))
                for i in range(2):
                    sp.wait_ge(rw_stored[i], 16 * (NB * HEADS // 2 + 1))
                    sp.wait_ge(lh_stored[i], 32 * (NB * HEADS // 2 + 1))

            @block.gpsimd
            def _(pool):
                pool.memset(mean_w[:, :], 1.0 / C).then_inc(const_done, 1)
                pool.memset(eps[:, :], EPS_C).then_inc(const_done, 1)

            @block.tensor
            def _(pe):
                def mean(tb, p):
                    pe.wait_ge(x_loaded[p], 16 * (tb // 2 + 1))
                    for c in range(CC):
                        mm = pe.matmul(mean_ps[:, :], mean_w[:, :], x_in[p][:, c, :], start=c == 0, stop=c == CC - 1)
                    mm.then_inc(mean_done, 1)

                def variance(tb):
                    pe.wait_ge(sq_done, tb + 1)
                    for c in range(CC):
                        mm = pe.matmul(var_ps[:, :], mean_w[:, :], sq[:, c, :], start=c == 0, stop=c == CC - 1)
                    mm.then_inc(var_done, 1)

                def product(tb, p, idx):
                    r = idx % RING
                    pe.wait_ge(lo_done, tb * OUTS + idx + 1)
                    for c in range(CC):
                        if idx < 2 * HEADS:
                            o = slice(idx * DH, (idx + 1) * DH)
                            mm = split_product(pe, bank[r][:, :], w_hi[:, c, o], w_lo[:, c, o],
                                               x_hi[p][:, c, :], x_lo[p][:, c, :], c == 0, c == CC - 1)
                        else:
                            t = slice((idx - 2 * HEADS) * P, (idx - 2 * HEADS + 1) * P)
                            mm = split_product(pe, bank[r][:, :], x_hi[p][:, c, t], x_lo[p][:, c, t],
                                               w_hi[:, c, 2 * C:], w_lo[:, c, 2 * C:], c == 0, c == CC - 1)
                    mm.then_inc(product_done, 1)

                def relative(tb, p, h):
                    u = tb * HEADS + h
                    pe.wait_ge(q_f_done, u + 1)
                    if h == 0:
                        pe.wait_ge(win_loaded[p], 16 * (tb // 2 + 1))
                    q = q_f[h % 2]
                    pe.wait_ge(rw_done, u + 1)
                    for k in range(TPB):
                        pe.matmul(rw_ps[:, k * P:(k + 1) * P], q[:, k * P:(k + 1) * P], rel_w[:, :],
                                  start=True, stop=True)
                    pe.wait_ge(lh_lo_done, u + 1)
                    for k in range(ROWS):
                        s = slice(k * SIDE, (k + 1) * SIDE)
                        mm = pe.matmul(lh_ps[0:SIDE, s], rel_h[:, p, ROWS - 1 - k:ROWS - 1 - k + SIDE], q[:, s],
                                       start=True, stop=True)
                    mm.then_inc(rel_done, 1)

                def one(tb, p, more):
                    pe.wait_ge(x_lo_done, tb + 1)
                    for idx in range(OUTS):
                        product(tb, p, idx)
                        if 1 <= idx <= HEADS:
                            relative(tb, p, idx - 1)
                        if more and idx == HEADS:
                            mean(tb + 1, 1 - p)
                        if more and idx == 2 * HEADS:
                            variance(tb + 1)

                pe.wait_ge(const_done, 2)
                mean(0, 0)
                variance(0)
                pe.wait_ge(w_lo_done, CC)
                pe.wait_ge(rel_loaded, 16)
                with pe.Fori(0, NB // 2 - 1) as m:
                    one(m * 2, 0, True)
                    one(m * 2 + 1, 1, True)
                one(NB - 2, 0, True)
                one(NB - 1, 1, False)

            @block.scalar
            def _(act):
                def square(tb):
                    act.wait_ge(xc_done, tb + 1)
                    act.activation(sq[:, :, :], xc[:, :, :], ACT.Square).then_inc(sq_done, 1)

                def deviation(tb):
                    act.wait_ge(var_done, tb + 1)
                    act.activation(dev[:, :], var_ps[:, :], ACT.Sqrt, bias=eps[:, 0:1]).then_inc(dev_done, 1)

                def norm_high(tb, p):
                    act.wait_ge(norm_step, 6 * (tb + 1))
                    act.activation(x_hi[p][:, :, :], xc[:, :, :], ACT.Copy).then_inc(x_hi_done, 1)

                def high(tb, idx):
                    r = idx % RING
                    act.wait_ge(product_done, tb * OUTS + idx + 1)
                    act.wait_ge(out_stored[r], (tb * PER + idx // RING + 1) * 32)
                    if idx < HEADS:
                        act.wait_ge(rel_done, tb * HEADS + idx + 1)
                        if idx >= 2:
                            act.wait_ge(lo_done, tb * OUTS + idx + 1 - 2 + RING)
                        act.activation(q_f[idx % 2][:, :], bank[r][:, :], ACT.Copy, scale=SCALE).then_inc(q_f_done, 1)
                        act.activation(outs[r][:, 0, :], bank[r][:, :], ACT.Copy, scale=SCALE).then_inc(hi_done, 1)
                    else:
                        act.activation(outs[r][:, 0, :], bank[r][:, :], ACT.Copy).then_inc(hi_done, 1)

                def relative(tb, h):
                    i, u = h % 2, tb * HEADS + h
                    act.wait_ge(rel_done, u + 1 + 2)
                    act.wait_ge(rw_stored[i], (tb * (HEADS // 2) + h // 2 + 1) * 16)
                    act.activation(rw[i][:, :], rw_ps[:, :], ACT.Copy).then_inc(rw_done, 1)
                    act.wait_ge(lh_stored[i], (tb * (HEADS // 2) + h // 2 + 1) * 32)
                    act.activation(lh[i][:, 0, :], lh_ps[0:SIDE, :], ACT.Copy).then_inc(lh_hi_done, 1)

                def one(tb, p, more):
                    for idx in range(OUTS):
                        high(tb, idx)
                        if 1 <= idx <= HEADS:
                            relative(tb, idx - 1)
                        if more and idx == HEADS + 2:
                            square(tb + 1)
                        if more and idx == 2 * HEADS:
                            deviation(tb + 1)
                        if more and idx == 2 * HEADS + 2:
                            norm_high(tb + 1, 1 - p)

                act.wait_ge(const_done, 2)
                square(0)
                deviation(0)
                norm_high(0, 0)
                for c in range(CC):
                    act.wait_ge(w_loaded, 16 * CC)
                    act.activation(w_hi[:, c, :], w_raw[:, c, :], ACT.Copy).then_inc(w_hi_done, 1)
                with act.Fori(0, NB // 2 - 1) as m:
                    one(m * 2, 0, True)
                    one(m * 2 + 1, 1, True)
                one(NB - 2, 0, True)
                one(NB - 1, 1, False)

            @block.vector
            def _(dve):
                def centre(tb, p):
                    dve.wait_ge(x_loaded[p], 16 * (tb // 2 + 1))
                    dve.wait_ge(mean_done, tb + 1)
                    dve.tensor_tensor(xc[:, :, :], x_in[p][:, :, :],
                                      mean_ps[:, :].unsqueeze(1).to_broadcast([P, CC, B]),
                                      ALU.subtract).then_inc(xc_done, 1)

                def normalise(tb):
                    n = tb * 6
                    dve.wait_ge(dev_done, tb + 1)
                    dve.reciprocal(rstd[:, :], dev[:, :]).then_inc(norm_step, 1)
                    dve.wait_ge(norm_step, n + 1)
                    dve.tensor_tensor(newton[:, :], rstd[:, :], rstd[:, :], ALU.mult).then_inc(norm_step, 1)
                    dve.wait_ge(norm_step, n + 2)
                    dve.scalar_tensor_tensor(out=newton[:, :], in0=var_ps[:, :], scalar=EPS_C, in1=newton[:, :],
                                             op0=ALU.add, op1=ALU.mult).then_inc(norm_step, 1)
                    dve.wait_ge(norm_step, n + 3)
                    dve.tensor_scalar(newton[:, :], newton[:, :], -0.5, 1.5, ALU.mult, ALU.add).then_inc(norm_step, 1)
                    dve.wait_ge(norm_step, n + 4)
                    dve.tensor_tensor(rstd[:, :], rstd[:, :], newton[:, :], ALU.mult).then_inc(norm_step, 1)
                    dve.wait_ge(norm_step, n + 5)
                    dve.tensor_tensor(xc[:, :, :], xc[:, :, :], rstd[:, :].unsqueeze(1).to_broadcast([P, CC, B]),
                                      ALU.mult).then_inc(norm_step, 1)

                def norm_low(tb, p):
                    dve.wait_ge(x_hi_done, tb + 1)
                    dve.tensor_tensor(x_lo[p][:, :, :], xc[:, :, :], f32(x_hi[p][:, :, :]), ALU.subtract) \
                       .then_inc(x_lo_done, 1)

                def low(tb, idx):
                    r = idx % RING
                    dve.wait_ge(hi_done, tb * OUTS + idx + 1)
                    whole = q_f[idx % 2] if idx < HEADS else bank[r]
                    dve.tensor_tensor(outs[r][:, 1, :], whole[:, :], f32(outs[r][:, 0, :]), ALU.subtract) \
                       .then_inc(lo_done, 1)

                def relative(tb, h):
                    u = tb * HEADS + h
                    dve.wait_ge(lh_hi_done, u + 1)
                    dve.tensor_tensor(lh[h % 2][:, 1, :], lh_ps[0:SIDE, :], f32(lh[h % 2][:, 0, :]), ALU.subtract) \
                       .then_inc(lh_lo_done, 1)

                def one(tb, p, more):
                    for idx in range(OUTS):
                        low(tb, idx)
                        if 1 <= idx <= HEADS:
                            relative(tb, idx - 1)
                        if more and idx == HEADS:
                            centre(tb + 1, 1 - p)
                        if more and idx == 2 * HEADS:
                            normalise(tb + 1)
                        if more and idx == 2 * HEADS + 2:
                            norm_low(tb + 1, 1 - p)

                centre(0, 0)
                normalise(0)
                norm_low(0, 0)
                for c in range(CC):
                    dve.wait_ge(w_hi_done, c + 1)
                    dve.tensor_tensor(w_lo[:, c, :], w_raw[:, c, :], f32(w_hi[:, c, :]), ALU.subtract) \
                       .then_inc(w_lo_done, 1)
                with dve.Fori(0, NB // 2 - 1) as m:
                    one(m * 2, 0, True)
                    one(m * 2 + 1, 1, True)
                one(NB - 2, 0, True)
                one(NB - 1, 1, False)


def attend(nc, sem, q_dram, k_dram, v_dram, rw_dram, attn_dram, ident_in, pick_in):
    NBLK = HEADS * NB
    CH = 1024
    CPT = T // CH
    STEPS = TPB * CPT
    JPC = CH // P
    PT = 4
    QUOTA = [0, 0, 4, 6, 6, 6, 5, 5]
    assert sum(QUOTA) == JT
    FIRST = [sum(QUOTA[:s]) for s in range(len(QUOTA))]

    with ExitStack() as ctx:
        def sb(name, shape, dt=F32):
            return ctx.enter_context(nc.sbuf_tensor(name, shape, dt))

        k_sb = sb("a_k", [P, 2, T], F32R)
        v_sb = sb("a_v", [P, 2, T], F32R)
        rows01 = [[sb(f"a_rows{par}{t}", [P, T]) for t in range(2)] for par in range(2)]
        rows23 = [sb(f"a_rows{t}", [P, T]) for t in range(2, TPB)]
        q_sb = [sb(f"a_q{i}", [P, 3, B], F32R) for i in range(2)]
        lw = [sb(f"a_lw{i}", [P, TPB, SIDE]) for i in range(2)]
        p_hi = [sb(f"a_phi{i}", [P, B], F32R) for i in range(PT)]
        p_lo = [sb(f"a_plo{i}", [P, B], F32R) for i in range(PT)]
        pick_f = sb("a_pick_f", [P, SIDE])
        pick = sb("a_pick", [P, SIDE], F32R)
        ident = sb("a_ident", [P, P])
        tops = sb("a_tops", [P, TPB, CPT])
        top = sb("a_top", [P, TPB])
        neg_top = sb("a_neg_top", [P, TPB])
        sums = [sb(f"a_sums{i}", [P, TPB, CPT]) for i in range(2)]
        total = sb("a_total", [P, TPB])
        inv = sb("a_inv", [P, TPB])
        o_t = sb("a_o_t", [P, B])
        o_out = sb("a_o_out", [P, TPB, DH])

        score_ps = [ctx.enter_context(nc.psum_tensor(f"a_score{i}", [P, CH], F32)) for i in range(2)]
        pt_ps = [ctx.enter_context(nc.psum_tensor(f"a_pt{i}", [P, B], F32)) for i in range(2)]
        o_ps = ctx.enter_context(nc.psum_tensor("a_o", [P, B], F32))
        turn_ps = ctx.enter_context(nc.psum_tensor("a_turn", [P, B], F32))

        passed = sem("a_passed")
        const_loaded = sem("a_const_loaded")
        pick_done = sem("a_pick_done")
        q_loaded = [sem(f"a_q_loaded{i}") for i in range(2)]
        lw_loaded = [sem(f"a_lw_loaded{i}") for i in range(2)]
        k_loaded = [sem(f"a_k_loaded{i}") for i in range(CPT)]
        v_loaded = [sem(f"a_v_loaded{i}") for i in range(CPT)]
        scored = sem("a_scored")
        biased = sem("a_biased")
        top_done = sem("a_top_done")
        neg_done = sem("a_neg_done")
        exp_done = sem("a_exp_done")
        turned = sem("a_turned")
        hi_done = sem("a_hi_done")
        lo_done = sem("a_lo_done")
        weighed = sem("a_weighed")
        o_copied = sem("a_o_copied")
        o_turned = sem("a_o_turned")
        total_done = sem("a_total_done")
        inv_done = sem("a_inv_done")
        o_done = sem("a_o_done")
        stored = sem("a_stored")
        o_out_free = sem("a_o_out_free")

        def rows(par, t):
            return rows01[par][t] if t < 2 else rows23[t - 2]

        def pick_cols(first_row, count):
            return pick[:, first_row:first_row + count].unsqueeze(2).to_broadcast([P, count, SIDE])

        def all_blocks(eng, pair, last_pair):
            with eng.Fori(0, NBLK // 2 - 1) as m:
                pair(m * 2)
            last_pair(NBLK - 2)

        with nc.Block() as block:

            @block.sync
            def _(sp):
                sp.sem_inc(biased, 2)
                sp.sem_inc(lo_done, 2)
                sp.sem_inc(weighed, PT)
                sp.sem_inc(o_copied, 1)
                sp.sem_inc(o_turned, 1)
                sp.sem_inc(o_done, TPB)
                sp.sem_inc(o_out_free, 1)
                sp.dma_start(ident[:, :], ident_in).then_inc(const_loaded, 16)
                sp.dma_start(pick_f[:, :], pick_in).then_inc(const_loaded, 16)

                def load_k(h, wait):
                    for c in range(CPT):
                        if wait:
                            sp.wait_ge(scored, h * NB * STEPS - CPT + c + 1)
                            own_wait(sp, passed)
                        sp.dma_start(f32(k_sb[:, :, c * CH:(c + 1) * CH]), k_dram[h, :, :, c * CH:(c + 1) * CH]) \
                          .then_inc(k_loaded[c], 16)

                def load_v(h, wait):
                    for c in range(CPT):
                        if wait:
                            sp.wait_ge(weighed, (h * NB - 1) * JT + (c + 1) * JPC + PT)
                            own_wait(sp, passed)
                        sp.dma_start(f32(v_sb[:, :, c * CH:(c + 1) * CH]), v_dram[h, :, :, c * CH:(c + 1) * CH]) \
                          .then_inc(v_loaded[c], 16)

                def load_q(h, b, par, wait):
                    if wait:
                        sp.wait_ge(biased, (h * NB + b - 1) * STEPS + 2)
                        own_wait(sp, passed)
                    sp.dma_start(f32(q_sb[par][:, :, :]), q_dram[h, :, :, bass.ds(b * B, B)]).then_inc(q_loaded[par], 16)
                    for xx in range(P // SIDE):
                        src = rw_dram[h, bass.ds(b * B, B), :].rearrange("(k x y) r -> x y k r", x=P // SIDE, y=SIDE)[xx]
                        skewed = bass.AP(src.tensor, src.offset + (SIDE - 1),
                                         [[P - 1, SIDE], [P * P, TPB], [1, SIDE]])
                        sp.dma_start(lw[par][xx * SIDE:(xx + 1) * SIDE, :, :], skewed).then_inc(lw_loaded[par], 16)

                load_q(0, 0, 0, False)
                load_k(0, False)
                load_q(0, 1, 1, False)
                load_v(0, False)

                def rest_of_head(h):
                    with sp.Fori(0, NB // 2 - 1) as i:
                        load_q(h, i * 2 + 2, 0, True)
                        load_q(h, i * 2 + 3, 1, True)

                rest_of_head(0)
                with sp.Fori(1, HEADS) as h:
                    load_q(h, 0, 0, True)
                    load_k(h, True)
                    load_q(h, 1, 1, True)
                    load_v(h, True)
                    rest_of_head(h)

            @block.gpsimd
            def _(pool):
                with pool.Fori(0, HEADS) as h:
                    with pool.Fori(0, NB) as b:
                        pool.wait_ge(o_done, (h * NB + b + 1) * TPB + TPB)
                        own_wait(pool, passed)
                        dst = attn_dram[bass.ds(b * B, B), bass.ds(h * DH, DH)].rearrange("(k p) d -> p k d", p=P)
                        pool.dma_start(dst, o_out[:, :, :]).then_inc(stored, 16)
                        pool.wait_ge(stored, (h * NB + b + 1) * 16)
                        pool.sem_inc(o_out_free, 1)

            @block.tensor
            def _(pe):
                def score(n, par, s):
                    t, c = divmod(s, CPT)
                    if s == 0:
                        pe.wait_ge(q_loaded[par], 16 * (n // 2 + 1))
                    if t == 0:
                        pe.wait_ge(k_loaded[c], 16 * (n // NB + 1))
                    pe.wait_ge(biased, n * STEPS + s + 1)
                    q = slice(t * P, (t + 1) * P)
                    for half in range(CH // B):
                        k = slice(c * CH + half * B, c * CH + (half + 1) * B)
                        out = score_ps[s % 2][:, half * B:(half + 1) * B]
                        pe.matmul(out, q_sb[par][:, 2, q], pick_cols(c * (CH // SIDE) + half * ROWS, ROWS),
                                  start=True, stop=False)
                        mm = split_product(pe, out, q_sb[par][:, 0, q], q_sb[par][:, 1, q],
                                           k_sb[:, 0, k], k_sb[:, 1, k], False, True)
                    mm.then_inc(scored, 1)

                def turn(n, par, j):
                    g = n * JT + j
                    if j % JPC == 0:
                        pe.wait_ge(exp_done, n * STEPS + STEPS - CPT + j // JPC + 1)
                    pe.wait_ge(lo_done, g + 1)
                    for t in range(TPB):
                        mm = pe.transpose(pt_ps[j % 2][:, t * P:(t + 1) * P], rows(par, t)[:, j * P:(j + 1) * P],
                                          ident[:, :])
                    mm.then_inc(turned, 1)

                def weigh(n, j):
                    g = n * JT + j
                    if j == 0:
                        pe.wait_ge(o_copied, n + 1)
                    if j % JPC == 0:
                        pe.wait_ge(v_loaded[j // JPC], 16 * (n // NB + 1))
                    pe.wait_ge(lo_done, g + 1 + 2)
                    split_product(pe, o_ps[:, :], v_sb[:, 0, j * P:(j + 1) * P], v_sb[:, 1, j * P:(j + 1) * P],
                                  p_hi[j % PT][:, :], p_lo[j % PT][:, :], j == 0, j == JT - 1).then_inc(weighed, 1)

                def turn_out(n):
                    pe.wait_ge(o_copied, n + 1 + 1)
                    pe.wait_ge(o_done, (n + 1) * TPB)
                    for t in range(TPB):
                        mm = pe.transpose(turn_ps[:, t * P:(t + 1) * P], o_t[:, t * P:(t + 1) * P], ident[:, :])
                    mm.then_inc(o_turned, 1)

                def values(n, par, s):
                    for j in range(FIRST[s], FIRST[s] + QUOTA[s]):
                        if j == 0:
                            turn(n, par, 0)
                        if j + 1 < JT:
                            turn(n, par, j + 1)
                        weigh(n, j)

                def first_half(n, par, prev):
                    for s in range(STEPS // 2):
                        score(n, par, s)
                        if prev:
                            values(n - 1, 1 - par, s)

                def second_half(n, par, prev):
                    for s in range(STEPS // 2, STEPS):
                        score(n, par, s)
                        if prev and s == STEPS // 2 + 1:
                            turn_out(n - 1)

                def pair(n):
                    first_half(n + 1, 1, True)
                    second_half(n + 1, 1, True)
                    first_half(n + 2, 0, True)
                    second_half(n + 2, 0, True)

                def last_pair(n):
                    first_half(n + 1, 1, True)
                    second_half(n + 1, 1, True)
                    for s in range(STEPS // 2):
                        values(n + 1, 1, s)
                    turn_out(n + 1)

                pe.wait_ge(pick_done, 1)
                first_half(0, 0, False)
                second_half(0, 0, False)
                all_blocks(pe, pair, last_pair)

            @block.scalar
            def _(act):
                def exponent(n, par, t, c):
                    if c == 0:
                        act.wait_ge(neg_done, n * TPB + t + 1)
                    row = rows(par, t)[:, c * CH:(c + 1) * CH]
                    act.activation(row, row, ACT.Exp, bias=neg_top[:, t:t + 1],
                                   accum_out=sums[par][:, t, c:c + 1]).then_inc(exp_done, 1)

                def high(n, j):
                    g = n * JT + j
                    act.wait_ge(turned, g + 1)
                    act.wait_ge(weighed, g + 1)
                    act.activation(p_hi[j % PT][:, :], pt_ps[j % 2][:, :], ACT.Copy).then_inc(hi_done, 1)

                def copy_out(n):
                    act.wait_ge(weighed, (n + 1) * JT + PT)
                    act.wait_ge(o_turned, n + 1)
                    act.activation(o_t[:, :], o_ps[:, :], ACT.Copy).then_inc(o_copied, 1)

                def highs(n, s):
                    for j in range(FIRST[s], FIRST[s] + QUOTA[s]):
                        if j == 0:
                            high(n, 0)
                        if j + 1 < JT:
                            high(n, j + 1)

                def block_steps(n, par, prev):
                    for s in range(STEPS):
                        t, c = divmod(s, CPT)
                        if prev and s < STEPS // 2:
                            highs(n - 1, s)
                        if prev and s == STEPS // 2:
                            copy_out(n - 1)
                        if t >= 1:
                            exponent(n, par, t - 1, c)

                def last_tile(n, par):
                    for c in range(CPT):
                        exponent(n, par, TPB - 1, c)

                def pair(n):
                    last_tile(n, 0)
                    block_steps(n + 1, 1, True)
                    last_tile(n + 1, 1)
                    block_steps(n + 2, 0, True)

                def last_pair(n):
                    last_tile(n, 0)
                    block_steps(n + 1, 1, True)
                    last_tile(n + 1, 1)
                    for s in range(STEPS // 2):
                        highs(n + 1, s)
                    copy_out(n + 1)

                act.wait_ge(const_loaded, 32)
                act.activation(pick[:, :], pick_f[:, :], ACT.Copy).then_inc(pick_done, 1)
                block_steps(0, 0, False)
                all_blocks(act, pair, last_pair)

            @block.vector
            def _(dve):
                def bias(n, par, s):
                    t, c = divmod(s, CPT)
                    if s == 0:
                        dve.wait_ge(lw_loaded[par], 32 * (n // 2 + 1))
                    dve.wait_ge(scored, n * STEPS + s + 1)
                    own_wait(dve, passed)
                    dve.tensor_tensor_reduce(
                        rows(par, t)[:, c * CH:(c + 1) * CH].rearrange("p (x y) -> p x y", y=SIDE),
                        score_ps[s % 2][:, :].rearrange("p (x y) -> p x y", y=SIDE),
                        lw[par][:, t, :].unsqueeze(1).to_broadcast([P, CH // SIDE, SIDE]),
                        1.0, -3.0e38, ALU.add, ALU.max, tops[:, t, c:c + 1]).then_inc(biased, 1)

                def maximum(n, t):
                    dve.wait_ge(biased, n * STEPS + (t + 1) * CPT + 2)
                    dve.tensor_reduce(top[:, t:t + 1], tops[:, t, :], AX.X, ALU.max).then_inc(top_done, 1)

                def negate(n, t):
                    dve.wait_ge(top_done, n * TPB + t + 1)
                    dve.tensor_scalar(neg_top[:, t:t + 1], top[:, t:t + 1], -1.0, None, ALU.mult) \
                       .then_inc(neg_done, 1)

                def low(n, j):
                    g = n * JT + j
                    dve.wait_ge(hi_done, g + 1)
                    dve.tensor_tensor(p_lo[j % PT][:, :], pt_ps[j % 2][:, :], f32(p_hi[j % PT][:, :]), ALU.subtract) \
                       .then_inc(lo_done, 1)

                def lows(n, s):
                    for j in range(FIRST[s], FIRST[s] + QUOTA[s]):
                        if j == 0:
                            low(n, 0)
                        if j + 1 < JT:
                            low(n, j + 1)

                def denominators(n, par):
                    dve.wait_ge(exp_done, (n + 1) * STEPS)
                    dve.tensor_reduce(total[:, :], sums[par][:, :, :], AX.X, ALU.add).then_inc(total_done, 1)
                    dve.wait_ge(total_done, n + 1)
                    dve.reciprocal(inv[:, :], total[:, :]).then_inc(inv_done, 1)

                def scale_out(n):
                    dve.wait_ge(inv_done, n + 1)
                    dve.wait_ge(o_turned, n + 1 + 1)
                    dve.wait_ge(o_out_free, n + 1)
                    for t in range(TPB):
                        dve.tensor_scalar(o_out[:, t, :], turn_ps[:, t * P:(t + 1) * P], inv[:, t:t + 1], None,
                                          ALU.mult).then_inc(o_done, 1)

                def block_steps(n, par, prev):
                    for s in range(STEPS):
                        t, c = divmod(s, CPT)
                        bias(n, par, s)
                        if c == CPT - 1:
                            maximum(n, t)
                        if prev and s < STEPS // 2:
                            lows(n - 1, s)
                        if c == CPT - 1:
                            negate(n, t)
                        if prev and s == STEPS // 2:
                            denominators(n - 1, 1 - par)
                        if prev and s == STEPS // 2 + 3:
                            scale_out(n - 1)

                def pair(n):
                    block_steps(n + 1, 1, True)
                    block_steps(n + 2, 0, True)

                def last_pair(n):
                    block_steps(n + 1, 1, True)
                    for s in range(STEPS // 2):
                        lows(n + 1, s)
                    denominators(n + 1, 1)
                    scale_out(n + 1)

                block_steps(0, 0, False)
                all_blocks(dve, pair, last_pair)


def bin_experts(nc, sem, attn_dram, x_t, w_bins, thr_in, ident_in, out):
    RING = 4
    with ExitStack() as ctx:
        def sb(name, shape, dt=F32):
            return ctx.enter_context(nc.sbuf_tensor(name, shape, dt))

        w_raw = [sb(f"f_w_raw{i}", [P, CC, C]) for i in range(2)]
        w_hi = [sb(f"f_w_hi{k}", [P, CC, C], F32R) for k in range(BINS)]
        w_lo = [sb(f"f_w_lo{k}", [P, CC, C], F32R) for k in range(BINS)]
        ident = sb("f_ident", [P, P])
        thr = sb("f_thr", [P, BINS - 1])
        eps = sb("f_eps", [P, 1])
        at = [sb(f"f_at{i}", [P, C]) for i in range(2)]
        xt = [sb(f"f_xt{i}", [P, C]) for i in range(2)]
        h1 = [sb(f"f_h1{i}", [P, C]) for i in range(2)]
        xf = sb("f_xf", [P, C])
        stats = sb("f_stats", [P, 6])
        mv = sb("f_mv", [P, 2])
        dev = sb("f_dev", [P, 1])
        rstd = sb("f_rstd", [P, 1])
        newton = sb("f_newton", [P, 1])
        above = sb("f_above", [P, BINS + 1])
        sel = [sb(f"f_sel{i}", [P, BINS]) for i in range(2)]
        xf_hi = [sb(f"f_xfhi{i}", [P, CC, P], F32R) for i in range(2)]
        xf_lo = [sb(f"f_xflo{i}", [P, CC, P], F32R) for i in range(2)]

        bank = [ctx.enter_context(nc.psum_tensor(f"f_bank{i}", [P, C], F32)) for i in range(RING)]
        turn_ps = [ctx.enter_context(nc.psum_tensor(f"f_turn{i}", [P, C], F32)) for i in range(2)]

        passed = sem("f_passed")
        const_loaded = sem("f_const_loaded")
        const_done = sem("f_const_done")
        w_loaded = [sem(f"f_w_loaded{i}") for i in range(2)]
        w_hi_done = sem("f_w_hi_done")
        w_lo_done = sem("f_w_lo_done")
        in_loaded = [sem(f"f_in_loaded{i}") for i in range(2)]
        norm_step = sem("f_norm_step")
        dev_done = sem("f_dev_done")
        turned = sem("f_turned")
        hi_done = sem("f_hi_done")
        lo_done = sem("f_lo_done")
        product_done = sem("f_product_done")
        acc_done = sem("f_acc_done")
        stored = [sem(f"f_stored{i}") for i in range(2)]
        NS = 12

        with nc.Block() as block:

            @block.sync
            def _(sp):
                sp.sem_inc(acc_done, RING)
                for i in range(2):
                    sp.sem_inc(stored[i], 16)
                sp.dma_start(ident[:, :], ident_in).then_inc(const_loaded, 16)
                sp.dma_start(thr[:, :], thr_in).then_inc(const_loaded, 16)

                def load_tile(t, i):
                    rows = bass.ds(t * P, P)
                    sp.dma_start(at[i][:, :], attn_dram[rows, :]).then_inc(in_loaded[i], 16)
                    sp.dma_start(xt[i][:, :], x_t[rows, :]).then_inc(in_loaded[i], 16)

                def store_tile(t, i):
                    sp.wait_ge(acc_done, (t + 1) * BINS + RING)
                    own_wait(sp, passed)
                    sp.dma_start(out[bass.ds(t * P, P), :], h1[i][:, :]).then_inc(stored[i], 16)

                load_tile(0, 0)
                load_tile(1, 1)
                for k in range(BINS):
                    if k >= 2:
                        sp.wait_ge(w_lo_done, k - 1)
                    sp.dma_start(w_raw[k % 2][:, :, :], w_bins[k].rearrange("(c p) n -> p c n", p=P)) \
                      .then_inc(w_loaded[k % 2], 16)

                def pair(t, more):
                    for i in range(2):
                        if more:
                            sp.wait_ge(norm_step, (t + i) * NS + 1)
                            own_wait(sp, passed)
                            load_tile(t + i + 2, i)
                        store_tile(t + i, i)

                with sp.Fori(0, JT // 2 - 1) as m:
                    pair(m * 2, True)
                pair(JT - 2, False)
                for i in range(2):
                    sp.wait_ge(stored[i], 16 * (JT // 2 + 1))

            @block.gpsimd
            def _(pool):
                pool.memset(eps[:, :], EPS_T).then_inc(const_done, 1)
                pool.memset(above[:, 0:1], 1.0).then_inc(const_done, 1)
                pool.memset(above[:, BINS:BINS + 1], 0.0).then_inc(const_done, 1)

            @block.tensor
            def _(pe):
                def turn(t, i):
                    pe.wait_ge(norm_step, t * NS + NS - 2)
                    for c in range(CC):
                        mm = pe.transpose(turn_ps[i][:, c * P:(c + 1) * P], xf[:, c * P:(c + 1) * P], ident[:, :])
                    mm.then_inc(turned, 1)

                def products(t, i, bins, first):
                    for k in bins:
                        if first:
                            pe.wait_ge(w_lo_done, k + 1)
                        pe.wait_ge(acc_done, t * BINS + k + 1)
                        for c in range(CC):
                            mm = split_product(pe, bank[k % RING][:, :], xf_hi[i][:, c, :], xf_lo[i][:, c, :],
                                               w_hi[k][:, c, :], w_lo[k][:, c, :], c == 0, c == CC - 1)
                        mm.then_inc(product_done, 1)

                def tile(t, i, first, more):
                    pe.wait_ge(lo_done, t + 1)
                    products(t, i, range(BINS // 2), first)
                    if more:
                        turn(t + 1, 1 - i)
                    products(t, i, range(BINS // 2, BINS), first)

                pe.wait_ge(const_loaded, 32)
                turn(0, 0)
                tile(0, 0, True, True)
                with pe.Fori(0, JT // 2 - 1) as m:
                    tile(m * 2 + 1, 1, False, True)
                    tile(m * 2 + 2, 0, False, True)
                tile(JT - 1, 1, False, False)

            @block.scalar
            def _(act):
                def deviation(t):
                    act.wait_ge(norm_step, t * NS + 3)
                    act.activation(dev[:, :], mv[:, 1:2], ACT.Sqrt, bias=eps[:, 0:1]).then_inc(dev_done, 1)

                def high(t, i):
                    act.wait_ge(turned, t + 1)
                    act.activation(xf_hi[i][:, :, :], turn_ps[i][:, :].rearrange("p (c t) -> p c t", c=CC), ACT.Copy) \
                       .then_inc(hi_done, 1)

                act.wait_ge(const_done, 3)
                deviation(0)
                high(0, 0)
                for k in range(BINS):
                    act.wait_ge(w_loaded[k % 2], 16 * (k // 2 + 1))
                    act.activation(w_hi[k][:, :, :], w_raw[k % 2][:, :, :], ACT.Copy).then_inc(w_hi_done, 1)
                deviation(1)
                high(1, 1)
                with act.Fori(0, JT // 2 - 1) as m:
                    for i in range(2):
                        deviation(m * 2 + 2 + i)
                        high(m * 2 + 2 + i, i)

            @block.vector
            def _(dve):
                def normalise(t, i):
                    n = t * NS
                    dve.wait_ge(in_loaded[i], 32 * (t // 2 + 1))
                    dve.wait_ge(stored[i], 16 * (t // 2 + 1))
                    dve.tensor_tensor(h1[i][:, :], at[i][:, :], xt[i][:, :], ALU.add).then_inc(norm_step, 1)
                    dve.wait_ge(norm_step, n + 1)
                    dve.bn_stats(stats[:, :], h1[i][:, :]).then_inc(norm_step, 1)
                    dve.wait_ge(norm_step, n + 2)
                    own_wait(dve, passed)
                    dve.bn_aggr(mv[:, :], stats[:, :]).then_inc(norm_step, 1)
                    dve.wait_ge(dev_done, t + 1)
                    dve.reciprocal(rstd[:, :], dev[:, :]).then_inc(norm_step, 1)
                    dve.wait_ge(norm_step, n + 4)
                    dve.tensor_tensor(newton[:, :], rstd[:, :], rstd[:, :], ALU.mult).then_inc(norm_step, 1)
                    dve.wait_ge(norm_step, n + 5)
                    dve.scalar_tensor_tensor(out=newton[:, :], in0=mv[:, 1:2], scalar=EPS_T, in1=newton[:, :],
                                             op0=ALU.add, op1=ALU.mult).then_inc(norm_step, 1)
                    dve.wait_ge(norm_step, n + 6)
                    dve.tensor_scalar(newton[:, :], newton[:, :], -0.5, 1.5, ALU.mult, ALU.add).then_inc(norm_step, 1)
                    dve.wait_ge(norm_step, n + 7)
                    dve.tensor_tensor(rstd[:, :], rstd[:, :], newton[:, :], ALU.mult).then_inc(norm_step, 1)
                    dve.wait_ge(norm_step, n + 8)
                    dve.tensor_scalar(xf[:, :], h1[i][:, :], mv[:, 0:1], rstd[:, 0:1], ALU.subtract, ALU.mult) \
                       .then_inc(norm_step, 1)
                    dve.wait_ge(norm_step, n + 9)
                    dve.tensor_scalar(above[:, 1:BINS], thr[:, :], xf[:, 0:1], None, ALU.is_lt).then_inc(norm_step, 1)
                    dve.wait_ge(norm_step, n + 10)
                    dve.tensor_tensor(sel[i][:, :], above[:, 0:BINS], above[:, 1:BINS + 1], ALU.subtract) \
                       .then_inc(norm_step, 1)
                    dve.engine_nop().then_inc(norm_step, 1)

                def low(t, i):
                    dve.wait_ge(hi_done, t + 1)
                    dve.tensor_tensor(xf_lo[i][:, :, :], turn_ps[i][:, :].rearrange("p (c t) -> p c t", c=CC),
                                      f32(xf_hi[i][:, :, :]), ALU.subtract).then_inc(lo_done, 1)

                def add_up(t, i, bins):
                    for k in bins:
                        dve.wait_ge(product_done, t * BINS + k + 1)
                        dve.wait_ge(acc_done, t * BINS + k + RING)
                        dve.scalar_tensor_tensor(out=h1[i][:, :], in0=bank[k % RING][:, :], scalar=sel[i][:, k:k + 1],
                                                 in1=h1[i][:, :], op0=ALU.mult, op1=ALU.add).then_inc(acc_done, 1)

                def tile(t, i, more):
                    if more:
                        normalise(t + 1, 1 - i)
                    add_up(t, i, range(BINS // 2))
                    if more:
                        low(t + 1, 1 - i)
                    add_up(t, i, range(BINS // 2, BINS))

                dve.wait_ge(const_done, 3)
                dve.wait_ge(const_loaded, 32)
                normalise(0, 0)
                low(0, 0)
                for k in range(BINS):
                    dve.wait_ge(w_hi_done, k + 1)
                    dve.tensor_tensor(w_lo[k][:, :, :], w_raw[k % 2][:, :, :], f32(w_hi[k][:, :, :]), ALU.subtract) \
                       .then_inc(w_lo_done, 1)
                with dve.Fori(0, JT // 2 - 1) as m:
                    tile(m * 2, 0, True)
                    tile(m * 2 + 1, 1, True)
                tile(JT - 2, 0, True)
                tile(JT - 1, 1, False)


def metaformer_block(nc, x, x_t, w_qkv_t, rel_w_t, rel_h_t, w_bins, ident, pick, thresholds, out):
    def dram(name, shape):
        return nc.dram_tensor(name, shape, F32, kind="Internal").ap()

    q_dram = dram("q_halves", [HEADS, P, 3, T])
    k_dram = dram("k_halves", [HEADS, P, 2, T])
    v_dram = dram("v_halves", [HEADS, P, 2, JT * DH])
    rw_dram = dram("rel_w_products", [HEADS, T, P])
    attn_dram = dram("attention", [T, C])

    with ExitStack() as ctx:
        def sem(name):
            return ctx.enter_context(nc.semaphore(name))

        project(nc, sem, x, w_qkv_t, rel_w_t, rel_h_t, q_dram, k_dram, v_dram, rw_dram)
        attend(nc, sem, q_dram, k_dram, v_dram, rw_dram, attn_dram, ident, pick)
        bin_experts(nc, sem, attn_dram, x_t, w_bins, thresholds, ident, out)


def kernel(x, L0_conv_w_qkv, L0_conv_rel_height, L0_conv_rel_width, L0_ffn_W):
    import numpy as np
    import concourse.bacc as bacc
    from concourse.bass_utils import run_bass_kernel_spmd

    x = np.asarray(x).reshape(C, T)
    rel_w = np.zeros((P, P), np.float32)
    rel_w[:, :2 * SIDE - 1] = np.asarray(L0_conv_rel_width).T
    arrays = {
        "x": np.ascontiguousarray(x),
        "x_t": np.ascontiguousarray(x.T),
        "w_qkv_t": np.ascontiguousarray(np.asarray(L0_conv_w_qkv).T),
        "rel_w_t": rel_w,
        "rel_h_t": np.ascontiguousarray(np.asarray(L0_conv_rel_height).T),
        "w_bins": np.ascontiguousarray(np.asarray(L0_ffn_W)),
        "ident": np.eye(P, dtype=np.float32),
        "pick": np.concatenate([np.eye(SIDE, dtype=np.float32)] * 2, axis=0),
        "thresholds": np.tile(np.array(THRESHOLDS, np.float32), (P, 1)),
    }
    nc = bacc.Bacc("TRN2", target_bir_lowering=False, num_devices=1)
    ins = [nc.dram_tensor(name, a.shape, F32, kind="ExternalInput").ap() for name, a in arrays.items()]
    out = nc.dram_tensor("out", (T, C), F32, kind="ExternalOutput").ap()
    metaformer_block(nc, *ins, out)
    result = run_bass_kernel_spmd(nc, [arrays], core_ids=[0]).results[0]["out"]
    return np.ascontiguousarray(result.T).reshape(1, C, SIDE, SIDE)
```

```python
from contextlib import ExitStack

import concourse.bass as bass
from concourse import mybir
from concourse.alu_op_type import AluOpType as ALU

P = 128
C = 512
CC = C // P
SIDE = 64
T = SIDE * SIDE
HEADS = 4
DH = C // HEADS
B = 512
NB = T // B
TPB = B // P
JT = T // P
BINS = 8
THRESHOLDS = [-1.5, -1.0, -0.5, 0.0, 0.5, 1.0, 1.5]
SCALE = DH ** -0.5
EPS_C = 1e-6
EPS_T = 1e-5
TILES = JT + BINS
LOG_P = P.bit_length() - 1
ROUTED = 33
REL = 2 * P

F32 = mybir.dt.float32
F32R = mybir.dt.float32r
I32 = mybir.dt.int32
ACT = mybir.ActivationFunctionType
AX = mybir.AxisListType


def f32(ap):
    return ap.bitcast(F32)


def own_wait(eng, passed):
    eng.sem_inc(passed, 1)


def split_product(pe, out, w_hi, w_lo, m_hi, m_lo, first, last):
    pe.matmul(out, w_lo, m_hi, start=first, stop=False)
    pe.matmul(out, w_hi, m_lo, start=False, stop=False)
    return pe.matmul(out, w_hi, m_hi, start=False, stop=last)


def project(nc, sem, x_t, w_qkv_t, rel_t, ident_in, q_dram, k_dram, v_dram, rel_dram):
    OUTS = 3 * HEADS
    RING = 4
    PER = OUTS // RING
    NORM = 2 * TPB + 5 + TPB

    with ExitStack() as ctx:
        def sb(name, shape, dt=F32):
            return ctx.enter_context(nc.sbuf_tensor(name, shape, dt))

        def ps(name, cols=B):
            return ctx.enter_context(nc.psum_tensor(name, [P, cols], F32))

        w_raw = [sb(f"p_w_raw{i}", [P, CC, C]) for i in range(3)]
        w_hi = [sb(f"p_w_hi{i}", [P, CC, C], F32R) for i in range(3)]
        w_lo = [sb(f"p_w_lo{i}", [P, CC, C], F32R) for i in range(3)]
        rel_raw = sb("p_rel_raw", [P, REL])
        rel_hi = sb("p_rel_hi", [P, REL], F32R)
        rel_lo = sb("p_rel_lo", [P, REL], F32R)
        ident = sb("p_ident", [P, P])
        eps = sb("p_eps", [P, 1])
        x_in = [sb(f"p_x{i}", [P, TPB, C]) for i in range(2)]
        xn = sb("p_xn", [P, TPB, C])
        stats = sb("p_stats", [P, TPB, 6])
        mv = sb("p_mv", [P, TPB, 2])
        dev = sb("p_dev", [P, TPB])
        rstd = sb("p_rstd", [P, TPB])
        newton = sb("p_newton", [P, TPB])
        x_hi = [sb(f"p_xhi{i}", [P, CC, B], F32R) for i in range(2)]
        x_lo = [sb(f"p_xlo{i}", [P, CC, B], F32R) for i in range(2)]
        q_f = [sb(f"p_qf{i}", [P, B]) for i in range(2)]
        outs = [sb(f"p_out{i}", [P, 2, B], F32R) for i in range(RING)]
        rel = [sb(f"p_rel{i}", [P, TPB, REL]) for i in range(2)]

        bank = [ps(f"p_bank{i}") for i in range(RING)]
        turn_ps = [ps(f"p_turn{i}") for i in range(2)]
        rel_ps = ps("p_relps", TPB * REL)

        passed = sem("p_passed")
        w_loaded = [sem(f"p_w_loaded{i}") for i in range(3)]
        small_loaded = sem("p_small_loaded")
        w_hi_done = sem("p_w_hi_done")
        w_lo_done = sem("p_w_lo_done")
        eps_done = sem("p_eps_done")
        x_loaded = [sem(f"p_x_loaded{i}") for i in range(2)]
        norm_step = sem("p_norm_step")
        dev_done = sem("p_dev_done")
        turned = sem("p_turned")
        x_hi_done = sem("p_x_hi_done")
        x_lo_done = sem("p_x_lo_done")
        product_done = sem("p_product_done")
        out_stored = [sem(f"p_out_stored{i}") for i in range(RING)]
        hi_done = sem("p_hi_done")
        lo_done = sem("p_lo_done")
        rel_done = sem("p_rel_done")
        rel_copied = sem("p_rel_copied")
        rel_stored = [sem(f"p_rel_stored{i}") for i in range(2)]

        with nc.Block() as block:

            def all_blocks(eng, one):
                with eng.Fori(0, NB // 2 - 1) as m:
                    one(m * 2, 0, True, True)
                    one(m * 2 + 1, 1, True, True)
                one(NB - 2, 0, True, False)
                one(NB - 1, 1, False, False)

            @block.sync
            def _(sp):
                sp.sem_inc(lo_done, RING)
                sp.sem_inc(x_lo_done, 2)
                sp.sem_inc(rel_copied, 1)
                for i in range(RING):
                    sp.sem_inc(out_stored[i], 32)
                for i in range(2):
                    sp.sem_inc(rel_stored[i], 16)

                def load_x(tb, p):
                    sp.dma_start(x_in[p][:, :, :], x_t[bass.ds(tb * B, B), :].rearrange("(t p) c -> p t c", p=P)) \
                      .then_inc(x_loaded[p], 16)

                load_x(0, 0)
                sp.dma_start(ident[:, :], ident_in).then_inc(small_loaded, 16)
                sp.dma_start(rel_raw[:, :], rel_t).then_inc(small_loaded, 16)
                for i in range(3):
                    sp.dma_start(w_raw[i][:, :, :], w_qkv_t[:, i * C:(i + 1) * C].rearrange("(c p) o -> p c o", p=P)) \
                      .then_inc(w_loaded[i], 16)
                load_x(1, 1)

                def store_out(tb, idx):
                    r = idx % RING
                    sp.wait_ge(lo_done, tb * OUTS + idx + 1 + RING)
                    own_wait(sp, passed)
                    cols = bass.ds(tb * B, B)
                    for half in range(2):
                        src = f32(outs[r][:, half, :])
                        if idx < HEADS:
                            dst = q_dram[idx, :, half, cols]
                        elif idx < 2 * HEADS:
                            dst = k_dram[idx - HEADS, :, half, cols]
                        else:
                            jt = tb * TPB + idx - 2 * HEADS
                            dst = v_dram[:, :, half, bass.ds(jt * DH, DH)].rearrange("h p d -> p h d")
                            src = src.rearrange("p (h d) -> p h d", h=HEADS)
                        sp.dma_start(dst, src).then_inc(out_stored[r], 16)

                def store_rel(tb, h):
                    i = h % 2
                    sp.wait_ge(rel_copied, tb * HEADS + h + 1 + 1)
                    own_wait(sp, passed)
                    dst = rel_dram[h, bass.ds(tb * B, B), :].rearrange("(k p) r -> p k r", p=P)
                    sp.dma_start(dst, rel[i][:, :, :]).then_inc(rel_stored[i], 16)

                def one(tb, p, more, more2):
                    for idx in range(OUTS):
                        store_out(tb, idx)
                        if 1 <= idx <= HEADS:
                            store_rel(tb, idx - 1)
                    if more2:
                        sp.wait_ge(norm_step, (tb + 1) * NORM)
                        own_wait(sp, passed)
                        load_x(tb + 2, p)

                all_blocks(sp, one)
                for i in range(RING):
                    sp.wait_ge(out_stored[i], 32 * (NB * PER + 1))
                for i in range(2):
                    sp.wait_ge(rel_stored[i], 16 * (NB * HEADS // 2 + 1))

            @block.gpsimd
            def _(pool):
                pool.memset(eps[:, :], EPS_C).then_inc(eps_done, 1)

            @block.tensor
            def _(pe):
                def turn(tb, t):
                    pe.wait_ge(norm_step, tb * NORM + NORM - TPB + t + 1)
                    pe.wait_ge(x_lo_done, tb * TPB + t + 1)
                    for c in range(CC):
                        mm = pe.transpose(turn_ps[t % 2][:, c * P:(c + 1) * P], xn[:, t, c * P:(c + 1) * P], ident[:, :])
                    mm.then_inc(turned, 1)

                def product(tb, p, idx):
                    r = idx % RING
                    pe.wait_ge(lo_done, tb * OUTS + idx + 1)
                    part, o = divmod(idx, HEADS)
                    own = slice(o * P, (o + 1) * P)
                    for c in range(CC):
                        if part < 2:
                            w, m = (w_hi[part][:, c, own], w_lo[part][:, c, own]), (x_hi[p][:, c, :], x_lo[p][:, c, :])
                        else:
                            w, m = (x_hi[p][:, c, own], x_lo[p][:, c, own]), (w_hi[2][:, c, :], w_lo[2][:, c, :])
                        mm = split_product(pe, bank[r][:, :], *w, *m, c == 0, c == CC - 1)
                    mm.then_inc(product_done, 1)

                def relative(tb, h):
                    pe.wait_ge(lo_done, tb * OUTS + h + 1 + RING)
                    pe.wait_ge(rel_copied, tb * HEADS + h + 1)
                    for k in range(TPB):
                        t = slice(k * P, (k + 1) * P)
                        mm = split_product(pe, rel_ps[:, k * REL:(k + 1) * REL], outs[h][:, 0, t], outs[h][:, 1, t],
                                           rel_hi[:, :], rel_lo[:, :], True, True)
                    mm.then_inc(rel_done, 1)

                def one(tb, p, more, more2, first=False):
                    pe.wait_ge(x_lo_done, (tb + 1) * TPB + 2)
                    for idx in range(OUTS):
                        if first and idx % HEADS == 0:
                            pe.wait_ge(w_lo_done, 2 + idx // HEADS)
                        product(tb, p, idx)
                        if 1 <= idx <= HEADS:
                            relative(tb, idx - 1)
                        if more and idx >= OUTS - 1 - TPB and idx < OUTS - 1:
                            turn(tb + 1, idx - (OUTS - 1 - TPB))

                pe.wait_ge(small_loaded, 32)
                for t in range(TPB):
                    turn(0, t)
                pe.wait_ge(w_lo_done, 4)
                all_blocks(pe, one)

            @block.scalar
            def _(act):
                def deviation(tb):
                    act.wait_ge(norm_step, tb * NORM + 2 * TPB)
                    act.activation(dev[:, :], mv[:, :, 1], ACT.Sqrt, bias=eps[:, 0:1]).then_inc(dev_done, 1)

                def norm_high(tb, p, t):
                    act.wait_ge(turned, tb * TPB + t + 1)
                    act.activation(x_hi[p][:, :, t * P:(t + 1) * P],
                                   turn_ps[t % 2][:, :].rearrange("p (c t) -> p c t", c=CC), ACT.Copy) \
                       .then_inc(x_hi_done, 1)

                def high(tb, idx):
                    r = idx % RING
                    act.wait_ge(product_done, tb * OUTS + idx + 1)
                    act.wait_ge(out_stored[r], (tb * PER + idx // RING + 1) * 32)
                    if idx < HEADS:
                        if idx >= 2:
                            act.wait_ge(lo_done, tb * OUTS + idx + 1 - 2 + RING)
                        act.activation(q_f[idx % 2][:, :], bank[r][:, :], ACT.Copy, scale=SCALE)
                        act.activation(outs[r][:, 0, :], bank[r][:, :], ACT.Copy, scale=SCALE).then_inc(hi_done, 1)
                    else:
                        if idx < 2 * HEADS:
                            act.wait_ge(rel_done, tb * HEADS + idx - HEADS + 1)
                        act.activation(outs[r][:, 0, :], bank[r][:, :], ACT.Copy).then_inc(hi_done, 1)

                def relative(tb, h):
                    i = h % 2
                    act.wait_ge(rel_done, tb * HEADS + h + 1)
                    act.wait_ge(rel_stored[i], (tb * (HEADS // 2) + h // 2 + 1) * 16)
                    act.activation(rel[i][:, :, :], rel_ps[:, :].rearrange("p (k r) -> p k r", k=TPB), ACT.Copy) \
                       .then_inc(rel_copied, 1)

                def one(tb, p, more, more2):
                    for idx in range(OUTS):
                        high(tb, idx)
                        if 1 <= idx <= HEADS:
                            relative(tb, idx - 1)
                        if more and idx == HEADS + 1:
                            deviation(tb + 1)
                        if more and idx >= OUTS - 1 - TPB and idx < OUTS - 1:
                            norm_high(tb + 1, 1 - p, idx - (OUTS - 1 - TPB))

                act.wait_ge(eps_done, 1)
                deviation(0)
                act.wait_ge(small_loaded, 32)
                act.activation(rel_hi[:, :], rel_raw[:, :], ACT.Copy).then_inc(w_hi_done, 1)
                for t in range(TPB):
                    norm_high(0, 0, t)
                for i in range(3):
                    act.wait_ge(w_loaded[i], 16)
                    act.activation(w_hi[i][:, :, :], w_raw[i][:, :, :], ACT.Copy).then_inc(w_hi_done, 1)
                all_blocks(act, one)

            @block.vector
            def _(dve):
                def statistics(tb, p):
                    n = tb * NORM
                    dve.wait_ge(x_loaded[p], 16 * (tb // 2 + 1))
                    for t in range(TPB):
                        dve.bn_stats(stats[:, t, :], x_in[p][:, t, :]).then_inc(norm_step, 1)
                    for t in range(TPB):
                        dve.wait_ge(norm_step, n + TPB + t)
                        own_wait(dve, passed)
                        dve.bn_aggr(mv[:, t, :], stats[:, t, :]).then_inc(norm_step, 1)

                def normalise(tb, p):
                    n = tb * NORM + 2 * TPB
                    dve.wait_ge(dev_done, tb + 1)
                    dve.reciprocal(rstd[:, :], dev[:, :]).then_inc(norm_step, 1)
                    dve.wait_ge(norm_step, n + 1)
                    dve.tensor_tensor(newton[:, :], rstd[:, :], rstd[:, :], ALU.mult).then_inc(norm_step, 1)
                    dve.wait_ge(norm_step, n + 2)
                    dve.scalar_tensor_tensor(out=newton[:, :], in0=mv[:, :, 1], scalar=EPS_C, in1=newton[:, :],
                                             op0=ALU.add, op1=ALU.mult).then_inc(norm_step, 1)
                    dve.wait_ge(norm_step, n + 3)
                    dve.tensor_scalar(newton[:, :], newton[:, :], -0.5, 1.5, ALU.mult, ALU.add).then_inc(norm_step, 1)
                    dve.wait_ge(norm_step, n + 4)
                    dve.tensor_tensor(rstd[:, :], rstd[:, :], newton[:, :], ALU.mult).then_inc(norm_step, 1)
                    dve.wait_ge(norm_step, n + 5)
                    for t in range(TPB):
                        dve.tensor_scalar(xn[:, t, :], x_in[p][:, t, :], mv[:, t, 0:1], rstd[:, t:t + 1],
                                          ALU.subtract, ALU.mult).then_inc(norm_step, 1)

                def norm_low(tb, p, t):
                    dve.wait_ge(x_hi_done, tb * TPB + t + 1)
                    own = x_lo[p][:, :, t * P:(t + 1) * P], x_hi[p][:, :, t * P:(t + 1) * P]
                    dve.tensor_tensor(own[0], turn_ps[t % 2][:, :].rearrange("p (c t) -> p c t", c=CC), f32(own[1]),
                                      ALU.subtract).then_inc(x_lo_done, 1)

                def low(tb, idx):
                    r = idx % RING
                    dve.wait_ge(hi_done, tb * OUTS + idx + 1)
                    whole = q_f[idx % 2] if idx < HEADS else bank[r]
                    dve.tensor_tensor(outs[r][:, 1, :], whole[:, :], f32(outs[r][:, 0, :]), ALU.subtract) \
                       .then_inc(lo_done, 1)

                def one(tb, p, more, more2):
                    for idx in range(OUTS):
                        low(tb, idx)
                        if more and idx == HEADS - 1:
                            statistics(tb + 1, 1 - p)
                        if more and idx == HEADS + 2:
                            normalise(tb + 1, 1 - p)
                        if more and idx >= OUTS - 1 - TPB and idx < OUTS - 1:
                            norm_low(tb + 1, 1 - p, idx - (OUTS - 1 - TPB))

                statistics(0, 0)
                normalise(0, 0)
                dve.wait_ge(w_hi_done, 1)
                dve.tensor_tensor(rel_lo[:, :], rel_raw[:, :], f32(rel_hi[:, :]), ALU.subtract).then_inc(w_lo_done, 1)
                for t in range(TPB):
                    norm_low(0, 0, t)
                for i in range(3):
                    dve.wait_ge(w_hi_done, i + 2)
                    dve.tensor_tensor(w_lo[i][:, :, :], w_raw[i][:, :, :], f32(w_hi[i][:, :, :]), ALU.subtract) \
                       .then_inc(w_lo_done, 1)
                all_blocks(dve, one)


def attend(nc, sem, q_dram, k_dram, v_dram, rel_dram, x_t, h1_dram, stats, first, ident_in):
    NBLK = HEADS * NB
    CH = 1024
    CPT = T // CH
    STEPS = TPB * CPT
    JPC = CH // P
    PT = 4
    BANKS = 3
    AHEAD = BANKS - 1
    QUOTA = [0, 0, 0] + [4] * 8
    FIRST = [sum(QUOTA[:s]) for s in range(len(QUOTA))]
    assert sum(QUOTA) == JT
    assert all(FIRST[2 * CPT + c] >= (c + 1) * JPC for c in range(CPT - 1))
    OUT = len(QUOTA)

    with ExitStack() as ctx:
        def sb(name, shape, dt=F32):
            return ctx.enter_context(nc.sbuf_tensor(name, shape, dt))

        k_sb = sb("a_k", [P, 2, T], F32R)
        v_sb = sb("a_v", [P, 2, T], F32R)
        rows01 = [[sb(f"a_rows{par}{t}", [P, T]) for t in range(2)] for par in range(2)]
        rows23 = [sb(f"a_rows{t}", [P, T]) for t in range(2, TPB)]
        q_sb = [sb(f"a_q{i}", [P, 2, B], F32R) for i in range(2)]
        lw = [sb(f"a_lw{i}", [P, TPB, SIDE]) for i in range(2)]
        lh = [sb(f"a_lh{i}", [P, TPB, SIDE]) for i in range(2)]
        pos = [sb(f"a_pos{i}", [P, CH]) for i in range(2)]
        p_hi = [sb(f"a_phi{i}", [P, B], F32R) for i in range(PT)]
        p_lo = [sb(f"a_plo{i}", [P, B], F32R) for i in range(PT)]
        ident = sb("a_ident", [P, P])
        tops = sb("a_tops", [P, TPB, CPT])
        top = sb("a_top", [P, TPB])
        neg_top = sb("a_neg_top", [P, TPB])
        sums = [sb(f"a_sums{i}", [P, TPB, CPT]) for i in range(2)]
        total = sb("a_total", [P, TPB])
        inv = sb("a_inv", [P, TPB])
        o_t = sb("a_o_t", [P, B])
        x_own = sb("a_x_own", [P, TPB, DH])
        o_out = sb("a_o_out", [P, TPB, DH])

        score_ps = [ctx.enter_context(nc.psum_tensor(f"a_score{i}", [P, CH], F32)) for i in range(2)]
        pt_ps = [ctx.enter_context(nc.psum_tensor(f"a_pt{i}", [P, B], F32)) for i in range(BANKS)]
        o_ps = ctx.enter_context(nc.psum_tensor("a_o", [P, B], F32))
        turn_ps = pt_ps[0]

        passed = sem("a_passed")
        const_loaded = sem("a_const_loaded")
        q_loaded = [sem(f"a_q_loaded{i}") for i in range(2)]
        bias_loaded = [sem(f"a_bias_loaded{i}") for i in range(2)]
        x_loaded = sem("a_x_loaded")
        k_loaded = [sem(f"a_k_loaded{i}") for i in range(CPT)]
        v_loaded = [sem(f"a_v_loaded{i}") for i in range(CPT)]
        scored = sem("a_scored")
        pos_done = sem("a_pos_done")
        biased = sem("a_biased")
        top_done = sem("a_top_done")
        neg_done = sem("a_neg_done")
        exp_done = sem("a_exp_done")
        turned = sem("a_turned")
        hi_done = sem("a_hi_done")
        lo_done = sem("a_lo_done")
        weighed = sem("a_weighed")
        o_copied = sem("a_o_copied")
        o_turned = sem("a_o_turned")
        total_done = sem("a_total_done")
        inv_done = sem("a_inv_done")
        o_done = sem("a_o_done")
        o_seen = sem("a_o_seen")
        stored = sem("a_stored")

        def rows(par, t):
            return rows01[par][t] if t < 2 else rows23[t - 2]

        def all_blocks(eng, pair, last_pair):
            with eng.Fori(0, NBLK // 2 - 1) as m:
                pair(m * 2)
            last_pair(NBLK - 2)

        with nc.Block() as block:

            @block.sync
            def _(sp):
                sp.sem_inc(biased, 2)
                sp.sem_inc(weighed, PT)
                sp.sem_inc(o_copied, 1)
                sp.sem_inc(o_turned, 1)
                sp.sem_inc(o_done, TPB)
                sp.sem_inc(stored, 16)

                def load_k(h, wait):
                    for c in range(CPT):
                        if wait:
                            sp.wait_ge(scored, h * NB * STEPS - CPT + c + 1)
                            own_wait(sp, passed)
                        sp.dma_start(f32(k_sb[:, :, c * CH:(c + 1) * CH]), k_dram[h, :, :, c * CH:(c + 1) * CH]) \
                          .then_inc(k_loaded[c], 16)

                def load_v(h, wait):
                    for c in range(CPT):
                        if wait:
                            sp.wait_ge(weighed, (h * NB - 1) * JT + (c + 1) * JPC + PT)
                            own_wait(sp, passed)
                        sp.dma_start(f32(v_sb[:, :, c * CH:(c + 1) * CH]), v_dram[h, :, :, c * CH:(c + 1) * CH]) \
                          .then_inc(v_loaded[c], 16)

                def load_q(h, b, par, wait):
                    if wait:
                        sp.wait_ge(biased, (h * NB + b - 1) * STEPS + 2)
                        own_wait(sp, passed)
                    sp.dma_start(f32(q_sb[par][:, :, :]), q_dram[h, :, :, bass.ds(b * B, B)]).then_inc(q_loaded[par], 16)
                    for xx in range(P // SIDE):
                        own = slice(xx * SIDE, (xx + 1) * SIDE)
                        src = rel_dram[h, bass.ds(b * B, B), :].rearrange("(k x y) r -> x y k r", x=P // SIDE, y=SIDE)[xx]
                        by_column = bass.AP(src.tensor, src.offset + (SIDE - 1),
                                            [[REL - 1, SIDE], [P * REL, TPB], [1, SIDE]])
                        sp.dma_start(lw[par][own, :, :], by_column).then_inc(bias_loaded[par], 16)
                        by_row = bass.AP(src.tensor, src.offset + (P + SIDE - 1 - xx) - b * (B // SIDE),
                                         [[REL, SIDE], [P * REL - P // SIDE, TPB], [1, SIDE]])
                        sp.dma_start(lh[par][own, :, :], by_row).then_inc(bias_loaded[par], 16)

                def place(dram, h, b):
                    return dram[bass.ds(b * B, B), bass.ds(h * DH, DH)].rearrange("(k p) d -> p k d", p=P)

                def store_out(h, b):
                    sp.wait_ge(o_done, (h * NB + b + 1) * TPB + TPB)
                    own_wait(sp, passed)
                    sp.dma_start(place(h1_dram, h, b), o_out[:, :, :]).then_inc(stored, 16)

                def load_x(h, b):
                    sp.dma_start(x_own[:, :, :], place(x_t, h, b)).then_inc(x_loaded, 16)

                load_q(0, 0, 0, False)
                load_k(0, False)
                sp.dma_start(ident[:, :], ident_in).then_inc(const_loaded, 16)
                load_q(0, 1, 1, False)
                load_v(0, False)
                load_x(0, 0)

                def rest_of_head(h):
                    with sp.Fori(0, NB // 2 - 1) as i:
                        for u in range(2):
                            load_q(h, i * 2 + 2 + u, u, True)
                            store_out(h, i * 2 + u)
                            load_x(h, i * 2 + 1 + u)

                rest_of_head(0)
                with sp.Fori(1, HEADS) as h:
                    load_q(h, 0, 0, True)
                    store_out(h - 1, NB - 2)
                    load_x(h - 1, NB - 1)
                    load_k(h, True)
                    load_q(h, 1, 1, True)
                    load_v(h, True)
                    store_out(h - 1, NB - 1)
                    load_x(h, 0)
                    rest_of_head(h)
                store_out(HEADS - 1, NB - 2)
                load_x(HEADS - 1, NB - 1)
                store_out(HEADS - 1, NB - 1)
                sp.wait_ge(stored, (NBLK + 1) * 16)

            @block.gpsimd
            def _(pool):
                def positions(n, par):
                    for s in range(STEPS):
                        t, c = divmod(s, CPT)
                        if s == 0:
                            pool.wait_ge(bias_loaded[par], 64 * (n // 2 + 1))
                        pool.wait_ge(biased, n * STEPS + s + 1)
                        own_wait(pool, passed)
                        rows_of = slice(c * (CH // SIDE), (c + 1) * (CH // SIDE))
                        pool.tensor_tensor(
                            pos[s % 2][:, :].rearrange("p (x y) -> p x y", y=SIDE),
                            lw[par][:, t, :].unsqueeze(1).to_broadcast([P, CH // SIDE, SIDE]),
                            lh[par][:, t, rows_of].unsqueeze(2).to_broadcast([P, CH // SIDE, SIDE]),
                            ALU.add).then_inc(pos_done, 1)

                with pool.Fori(0, NBLK // 2) as m:
                    for par in range(2):
                        positions(m * 2 + par, par)

            @block.tensor
            def _(pe):
                def score(n, par, s):
                    t, c = divmod(s, CPT)
                    if s == 0:
                        pe.wait_ge(q_loaded[par], 16 * (n // 2 + 1))
                    if t == 0:
                        pe.wait_ge(k_loaded[c], 16 * (n // NB + 1))
                    pe.wait_ge(biased, n * STEPS + s + 1)
                    q = slice(t * P, (t + 1) * P)
                    for half in range(CH // B):
                        k = slice(c * CH + half * B, c * CH + (half + 1) * B)
                        out = score_ps[s % 2][:, half * B:(half + 1) * B]
                        mm = split_product(pe, out, q_sb[par][:, 0, q], q_sb[par][:, 1, q],
                                           k_sb[:, 0, k], k_sb[:, 1, k], True, True)
                    mm.then_inc(scored, 1)

                def turn(n, par, j):
                    g = n * JT + j
                    if j % JPC == 0:
                        pe.wait_ge(exp_done, n * STEPS + STEPS - CPT + j // JPC + 1)
                    if j == 0:
                        pe.wait_ge(o_done, (n + 1) * TPB)
                    if j >= BANKS:
                        pe.wait_ge(lo_done, g - BANKS + 1)
                    for t in range(TPB):
                        mm = pe.transpose(pt_ps[j % BANKS][:, t * P:(t + 1) * P], rows(par, t)[:, j * P:(j + 1) * P],
                                          ident[:, :])
                    mm.then_inc(turned, 1)

                def weigh(n, j):
                    g = n * JT + j
                    if j == 0:
                        pe.wait_ge(o_copied, n + 1)
                    if j % JPC == 0:
                        pe.wait_ge(v_loaded[j // JPC], 16 * (n // NB + 1))
                    pe.wait_ge(lo_done, g + 1)
                    split_product(pe, o_ps[:, :], v_sb[:, 0, j * P:(j + 1) * P], v_sb[:, 1, j * P:(j + 1) * P],
                                  p_hi[j % PT][:, :], p_lo[j % PT][:, :], j == 0, j == JT - 1).then_inc(weighed, 1)

                def turn_out(n):
                    pe.wait_ge(o_copied, n + 1 + 1)
                    for t in range(TPB):
                        mm = pe.transpose(turn_ps[:, t * P:(t + 1) * P], o_t[:, t * P:(t + 1) * P], ident[:, :])
                    mm.then_inc(o_turned, 1)

                def values(n, par, s):
                    for j in range(FIRST[s], FIRST[s] + QUOTA[s]):
                        if j == 0:
                            for first in range(AHEAD):
                                turn(n, par, first)
                        if j + AHEAD < JT:
                            turn(n, par, j + AHEAD)
                        weigh(n, j)

                def block_steps(n, par, prev):
                    for s in range(STEPS):
                        score(n, par, s)
                        if prev and s < OUT:
                            values(n - 1, 1 - par, s)
                        if prev and s == OUT + 1:
                            turn_out(n - 1)

                def pair(n):
                    block_steps(n + 1, 1, True)
                    block_steps(n + 2, 0, True)

                def last_pair(n):
                    block_steps(n + 1, 1, True)
                    for s in range(OUT):
                        values(n + 1, 1, s)
                    turn_out(n + 1)

                pe.wait_ge(const_loaded, 16)
                block_steps(0, 0, False)
                all_blocks(pe, pair, last_pair)

            @block.scalar
            def _(act):
                def exponent(n, par, t, c):
                    if c == 0:
                        act.wait_ge(neg_done, n * TPB + t + 1)
                    row = rows(par, t)[:, c * CH:(c + 1) * CH]
                    act.activation(row, row, ACT.Exp, bias=neg_top[:, t:t + 1],
                                   accum_out=sums[par][:, t, c:c + 1]).then_inc(exp_done, 1)

                def high(n, j):
                    g = n * JT + j
                    act.wait_ge(turned, g + 1)
                    act.wait_ge(weighed, g + 1)
                    act.activation(p_hi[j % PT][:, :], pt_ps[j % BANKS][:, :], ACT.Copy).then_inc(hi_done, 1)

                def copy_out(n):
                    act.wait_ge(weighed, (n + 1) * JT + PT)
                    act.wait_ge(o_turned, n + 1)
                    act.activation(o_t[:, :], o_ps[:, :], ACT.Copy).then_inc(o_copied, 1)

                def highs(n, s):
                    for j in range(FIRST[s], FIRST[s] + QUOTA[s]):
                        if j == 0:
                            for first in range(AHEAD):
                                high(n, first)
                        if j + AHEAD < JT:
                            high(n, j + AHEAD)

                def block_steps(n, par, prev):
                    for s in range(STEPS):
                        t, c = divmod(s, CPT)
                        if prev and s < OUT:
                            highs(n - 1, s)
                        if prev and s == OUT:
                            copy_out(n - 1)
                        if t >= 1:
                            exponent(n, par, t - 1, c)

                def last_tile(n, par):
                    for c in range(CPT):
                        exponent(n, par, TPB - 1, c)

                def pair(n):
                    last_tile(n, 0)
                    block_steps(n + 1, 1, True)
                    last_tile(n + 1, 1)
                    block_steps(n + 2, 0, True)

                def last_pair(n):
                    last_tile(n, 0)
                    block_steps(n + 1, 1, True)
                    last_tile(n + 1, 1)
                    for s in range(OUT):
                        highs(n + 1, s)
                    copy_out(n + 1)

                block_steps(0, 0, False)
                all_blocks(act, pair, last_pair)

            @block.vector
            def _(dve):
                def bias(n, par, s):
                    t, c = divmod(s, CPT)
                    dve.wait_ge(pos_done, n * STEPS + s + 1)
                    dve.wait_ge(scored, n * STEPS + s + 1)
                    own_wait(dve, passed)
                    dve.tensor_tensor_reduce(
                        rows(par, t)[:, c * CH:(c + 1) * CH], score_ps[s % 2][:, :], pos[s % 2][:, :],
                        1.0, -3.0e38, ALU.add, ALU.max, tops[:, t, c:c + 1]).then_inc(biased, 1)

                def maximum(n, t):
                    dve.wait_ge(biased, n * STEPS + (t + 1) * CPT + 2)
                    dve.tensor_reduce(top[:, t:t + 1], tops[:, t, :], AX.X, ALU.max).then_inc(top_done, 1)

                def negate(n, t):
                    dve.wait_ge(top_done, n * TPB + t + 1)
                    dve.tensor_scalar(neg_top[:, t:t + 1], top[:, t:t + 1], -1.0, None, ALU.mult) \
                       .then_inc(neg_done, 1)

                def low(n, j):
                    g = n * JT + j
                    dve.wait_ge(hi_done, g + 1)
                    dve.tensor_tensor(p_lo[j % PT][:, :], pt_ps[j % BANKS][:, :], f32(p_hi[j % PT][:, :]), ALU.subtract) \
                       .then_inc(lo_done, 1)

                def lows(n, s):
                    for j in range(FIRST[s], FIRST[s] + QUOTA[s]):
                        if j == 0:
                            for first in range(AHEAD):
                                low(n, first)
                        if j + AHEAD < JT:
                            low(n, j + AHEAD)

                def denominators(n, par):
                    dve.wait_ge(exp_done, (n + 1) * STEPS)
                    dve.tensor_reduce(total[:, :], sums[par][:, :, :], AX.X, ALU.add).then_inc(total_done, 1)
                    dve.wait_ge(total_done, n + 1)
                    dve.reciprocal(inv[:, :], total[:, :]).then_inc(inv_done, 1)

                def scale_out(n):
                    dve.wait_ge(inv_done, n + 1)
                    dve.wait_ge(o_turned, n + 1 + 1)
                    dve.wait_ge(x_loaded, 16 * (n + 1))
                    dve.wait_ge(stored, 16 * (n + 1))
                    for t in range(TPB):
                        dve.scalar_tensor_tensor(out=o_out[:, t, :], in0=turn_ps[:, t * P:(t + 1) * P],
                                                 scalar=inv[:, t:t + 1], in1=x_own[:, t, :], op0=ALU.mult,
                                                 op1=ALU.add).then_inc(o_done, 1)

                def statistics(n):
                    dve.wait_ge(o_done, (n + 2) * TPB)
                    own_wait(dve, passed)
                    for t in range(TPB):
                        dve.bn_stats(stats[:, bass.ds(n * TPB + t, 1), :].rearrange("p t s -> p (t s)"),
                                     o_out[:, t, :]).then_inc(o_seen, 1)
                    dve.tensor_copy(first[:, bass.ds(n * TPB, TPB)], o_out[:, :, 0]).then_inc(o_seen, 1)

                def block_steps(n, par, prev):
                    for s in range(STEPS):
                        t, c = divmod(s, CPT)
                        bias(n, par, s)
                        if c == CPT - 1:
                            maximum(n, t)
                        if prev and s < OUT:
                            lows(n - 1, s)
                        if c == CPT - 1:
                            negate(n, t)
                        if prev and s == OUT:
                            denominators(n - 1, 1 - par)
                        if prev and s == OUT + 2:
                            scale_out(n - 1)
                        if prev and s == OUT + 3:
                            statistics(n - 1)

                def pair(n):
                    block_steps(n + 1, 1, True)
                    block_steps(n + 2, 0, True)

                def last_pair(n):
                    block_steps(n + 1, 1, True)
                    for s in range(OUT):
                        lows(n + 1, s)
                    denominators(n + 1, 1)
                    scale_out(n + 1)
                    statistics(n + 1)

                block_steps(0, 0, False)
                all_blocks(dve, pair, last_pair)


def bin_experts(nc, sem, h1_dram, stats, first, w_bins, slots_dram, steps_in, tokens_in, tri_in, ident_in, out):
    RAW = 3
    RING = 4
    assert TILES % RING == 0
    INFO = 4

    with ExitStack() as ctx:
        def sb(name, shape, dt=F32):
            return ctx.enter_context(nc.sbuf_tensor(name, shape, dt))

        w_raw = [sb(f"f_w_raw{i}", [P, CC, C]) for i in range(RAW)]
        w_hi = sb("f_w_hi", [P, BINS, CC, C], F32R)
        w_lo = sb("f_w_lo", [P, BINS, CC, C], F32R)
        ident = sb("f_ident", [P, P])
        steps = sb("f_steps", [P, BINS - 1 + JT + TILES])
        thresholds = steps[:, 0:BINS - 1]
        full_tiles = steps[:, BINS - 1:BINS - 1 + JT]
        tile_numbers = steps[:, BINS - 1 + JT:]
        eps = sb("f_eps", [P, 1])
        tri_raw = sb("f_tri_raw", [P, 2 * P])
        tri = sb("f_tri", [P, 2 * P], F32R)

        mv = sb("f_mv", [P, JT, 2])
        dev = sb("f_dev", [P, JT])
        rstd = sb("f_rstd", [P, JT])
        newton = sb("f_newton", [P, JT])
        y = sb("f_y", [P, JT])
        above = sb("f_above", [P, BINS + 1, JT])
        in_bin = sb("f_in_bin", [P, BINS, JT], F32R)
        upto = [sb(f"f_upto{i}", [P, BINS, 2 * JT]) for i in range(2)]
        filled = sb("f_filled", [P, BINS, JT])
        ends = [sb(f"f_ends{i}", [P, 2 * BINS]) for i in range(2)]
        starts = sb("f_starts", [P, BINS])
        place = sb("f_place", [P, BINS, JT])
        slot_f = sb("f_slot_f", [P, JT])
        slot = sb("f_slot", [P, JT], I32)
        lane = sb("f_lane", [P, JT], I32)
        tile_of = sb("f_tile_of", [P, JT], I32)
        row = sb("f_row", [P, JT], I32)
        passed_ends = sb("f_passed_ends", [P, TILES, BINS - 1])
        tile_bin_f = sb("f_tile_bin_f", [P, TILES])
        tile_bin = sb("f_tile_bin", [P, TILES], I32)
        info = sb("f_info", [P, JT, INFO])
        pads = sb("f_pads", [P, TILES, INFO])
        slots = sb("f_slots", [P, TILES, INFO])
        from_row = [sb(f"f_from{i}", [P, 1], I32) for i in range(RING)]
        to_row = [sb(f"f_to{i}", [P, 1], I32) for i in range(RING)]
        h1 = [sb(f"f_h1{i}", [P, C]) for i in range(RING)]
        res = [sb(f"f_res{i}", [P, C]) for i in range(RING)]
        xf = [sb(f"f_xf{i}", [P, C]) for i in range(2)]
        xf_hi = [sb(f"f_xfhi{i}", [P, CC, P], F32R) for i in range(2)]
        xf_lo = [sb(f"f_xflo{i}", [P, CC, P], F32R) for i in range(2)]

        count_ps = ctx.enter_context(nc.psum_tensor("f_count", [P, 2, BINS * JT], F32))
        bank = [ctx.enter_context(nc.psum_tensor(f"f_bank{i}", [P, C], F32)) for i in range(2)]
        turn_ps = [ctx.enter_context(nc.psum_tensor(f"f_turn{i}", [P, C], F32)) for i in range(2)]

        passed = sem("f_passed")
        const_loaded = sem("f_const_loaded")
        set_done = sem("f_set_done")
        tri_done = sem("f_tri_done")
        pads_stored = sem("f_pads_stored")
        w_loaded = [sem(f"f_w_loaded{i}") for i in range(RAW)]
        w_hi_done = sem("f_w_hi_done")
        w_lo_done = sem("f_w_lo_done")
        stats_done = sem("f_stats_done")
        dev_done = sem("f_dev_done")
        route_step = sem("f_route_step")
        counted = sem("f_counted")
        bins_done = sem("f_bins_done")
        slots_filled = sem("f_slots_filled")
        slots_loaded = sem("f_slots_loaded")
        from_done = sem("f_from_done")
        gathered = [sem(f"f_gathered{i}") for i in range(RING)]
        xf_done = sem("f_xf_done")
        turned = sem("f_turned")
        hi_done = sem("f_hi_done")
        lo_done = sem("f_lo_done")
        product_done = sem("f_product_done")
        res_done = sem("f_res_done")
        scattered = [sem(f"f_scattered{i}") for i in range(RING)]

        def all_tiles(eng, one):
            for j in range(2 * RING):
                one(j, j % RING)
            with eng.Fori(2, TILES // RING - 1) as m:
                for i in range(RING):
                    one(m * RING + i, i, True, True)
            for i in range(RING):
                one(TILES - RING + i, i)

        with nc.Block() as block:

            @block.sync
            def _(sp):
                sp.dma_start(steps[:, :], steps_in).then_inc(const_loaded, 16)
                sp.dma_start(info[:, :, :], tokens_in).then_inc(const_loaded, 16)
                sp.dma_start(tri_raw[:, :], tri_in).then_inc(const_loaded, 16)
                sp.dma_start(ident[:, :], ident_in).then_inc(const_loaded, 16)

                def load_w(k):
                    if k >= RAW:
                        sp.wait_ge(w_lo_done, k - RAW + 1)
                    sp.dma_start(w_raw[k % RAW][:, :, :], w_bins[k].rearrange("(c p) n -> p c n", p=P)) \
                      .then_inc(w_loaded[k % RAW], 16)

                load_w(0)
                sp.wait_ge(set_done, 6)
                sp.dma_start(slots_dram.rearrange("(p j) i -> p j i", p=P), pads[:, :, :]).then_inc(pads_stored, 16)
                for k in range(1, BINS):
                    load_w(k)
                sp.wait_ge(slots_filled, 16 * JT)
                sp.dma_start(slots[:, :, :], slots_dram.rearrange("(p j) i -> p j i", p=P)).then_inc(slots_loaded, 16)

            @block.gpsimd
            def _(pool):
                pool.memset(pads[:, :, :], 0.0).then_inc(set_done, 1)
                pool.wait_ge(set_done, 1)
                pool.memset(pads[:, :, 0], float(T)).then_inc(set_done, 1)
                for i in range(2):
                    pool.memset(upto[i][:, :, 0:JT], 0.0).then_inc(set_done, 1)
                    pool.memset(ends[i][:, 0:BINS], 0.0).then_inc(set_done, 1)
                pool.memset(eps[:, :], EPS_T).then_inc(set_done, 1)
                pool.memset(above[:, 0, :], 1.0).then_inc(set_done, 1)
                pool.memset(above[:, BINS, :], 0.0).then_inc(set_done, 1)

                pool.wait_ge(pads_stored, 16)
                pool.wait_ge(route_step, ROUTED)
                for t in range(JT):
                    pool.indirect_dma_start(slots_dram, bass.IndirectOffsetOnAxis(row[:, t:t + 1], 0),
                                            info[:, t, :], None).then_inc(slots_filled, 16)

                def gather(j, i):
                    pool.wait_ge(from_done, j + 1)
                    own_wait(pool, passed)
                    pool.indirect_dma_start(h1[i][:, :], None, h1_dram, bass.IndirectOffsetOnAxis(from_row[i][:, :], 0)) \
                        .then_inc(gathered[i], 16)

                def scatter(j, i):
                    pool.indirect_dma_start(out, bass.IndirectOffsetOnAxis(to_row[i][:, :], 0), res[i][:, :], None,
                                            bounds_check=T - 1, oob_is_err=False).then_inc(scattered[i], 16)

                def one(j, i, before=False, after=False):
                    if before or j >= 1:
                        pool.wait_ge(res_done, j)
                        own_wait(pool, passed)
                        scatter(j - 1, (i - 1) % RING)
                    if after or j + RING - 1 < TILES:
                        gather(j + RING - 1, (i - 1) % RING)

                for j in range(RING - 1):
                    gather(j, j)
                all_tiles(pool, one)
                pool.wait_ge(res_done, TILES)
                scatter(TILES - 1, RING - 1)
                for i in range(RING):
                    pool.wait_ge(scattered[i], 16 * (TILES // RING))

            @block.tensor
            def _(pe):
                def turn(j, i):
                    pe.wait_ge(xf_done, j + 1)
                    for c in range(CC):
                        mm = pe.transpose(turn_ps[i % 2][:, c * P:(c + 1) * P], xf[i % 2][:, c * P:(c + 1) * P],
                                          ident[:, :])
                    mm.then_inc(turned, 1)

                def one(j, i, before=False, after=False):
                    if after or j + 1 < TILES:
                        turn(j + 1, i + 1)
                    bin_no = pe.value_load(tile_bin[0:1, bass.ds(j, 1)], min_val=0, max_val=BINS - 1)
                    pe.wait_ge(w_lo_done, bin_no + 1)
                    pe.wait_ge(lo_done, j + 1)
                    if before or j >= 2:
                        pe.wait_ge(res_done, j - 1)
                    for c in range(CC):
                        hi = w_hi[:, bass.ds(bin_no, 1), c, :].rearrange("p k n -> p (k n)")
                        lo = w_lo[:, bass.ds(bin_no, 1), c, :].rearrange("p k n -> p (k n)")
                        mm = split_product(pe, bank[i % 2][:, :], xf_hi[i % 2][:, c, :], xf_lo[i % 2][:, c, :],
                                           hi, lo, c == 0, c == CC - 1)
                    mm.then_inc(product_done, 1)

                pe.wait_ge(tri_done, 1)
                pe.wait_ge(bins_done, 1)
                for i in range(2):
                    pe.matmul(count_ps[:, i, :], tri[:, i * P:(i + 1) * P],
                              in_bin[:, :, :].rearrange("p k t -> p (k t)"), start=True, stop=True).then_inc(counted, 1)
                pe.wait_ge(const_loaded, 64)
                turn(0, 0)
                pe.wait_ge(route_step, ROUTED)
                all_tiles(pe, one)

            @block.scalar
            def _(act):
                def high(j, i, before=False, after=False):
                    act.wait_ge(turned, j + 1)
                    if before or j >= 2:
                        act.wait_ge(product_done, j - 1)
                    act.activation(xf_hi[i % 2][:, :, :], turn_ps[i % 2][:, :].rearrange("p (c t) -> p c t", c=CC),
                                   ACT.Copy).then_inc(hi_done, 1)

                act.wait_ge(set_done, 9)
                act.wait_ge(stats_done, JT)
                act.activation(dev[:, :], mv[:, :, 1], ACT.Sqrt, bias=eps[:, 0:1]).then_inc(dev_done, 1)
                act.wait_ge(const_loaded, 64)
                act.activation(tri[:, :], tri_raw[:, :], ACT.Copy).then_inc(tri_done, 1)
                for k in range(BINS):
                    act.wait_ge(w_loaded[k % RAW], 16 * (k // RAW + 1))
                    act.activation(w_hi[:, k, :, :], w_raw[k % RAW][:, :, :], ACT.Copy).then_inc(w_hi_done, 1)
                all_tiles(act, high)

            @block.vector
            def _(dve):
                def low_w(k):
                    dve.wait_ge(w_hi_done, k + 1)
                    dve.tensor_tensor(w_lo[:, k, :, :], w_raw[k % RAW][:, :, :], f32(w_hi[:, k, :, :]), ALU.subtract) \
                       .then_inc(w_lo_done, 1)

                for t in range(JT):
                    dve.bn_aggr(mv[:, t, :], stats[:, :, :].rearrange("p (h t) s -> p t h s", h=HEADS)[:, t, :, :]) \
                       .then_inc(stats_done, 1)
                dve.wait_ge(dev_done, 1)
                dve.reciprocal(rstd[:, :], dev[:, :]).then_inc(route_step, 1)
                dve.wait_ge(route_step, 1)
                dve.tensor_tensor(newton[:, :], rstd[:, :], rstd[:, :], ALU.mult).then_inc(route_step, 1)
                dve.wait_ge(route_step, 2)
                dve.scalar_tensor_tensor(out=newton[:, :], in0=mv[:, :, 1], scalar=EPS_T, in1=newton[:, :],
                                         op0=ALU.add, op1=ALU.mult).then_inc(route_step, 1)
                dve.wait_ge(route_step, 3)
                dve.tensor_scalar(newton[:, :], newton[:, :], -0.5, 1.5, ALU.mult, ALU.add).then_inc(route_step, 1)
                dve.wait_ge(route_step, 4)
                dve.tensor_tensor(rstd[:, :], rstd[:, :], newton[:, :], ALU.mult).then_inc(route_step, 1)
                dve.tensor_tensor(y[:, :], first[:, 0:JT], mv[:, :, 0], ALU.subtract).then_inc(route_step, 1)
                dve.wait_ge(route_step, 6)
                dve.tensor_tensor(y[:, :], y[:, :], rstd[:, :], ALU.mult).then_inc(route_step, 1)
                dve.wait_ge(route_step, 7)
                dve.wait_ge(set_done, 9)
                dve.wait_ge(const_loaded, 64)
                dve.tensor_tensor(above[:, 1:BINS, :], y[:, :].unsqueeze(1).to_broadcast([P, BINS - 1, JT]),
                                  thresholds.unsqueeze(2).to_broadcast([P, BINS - 1, JT]), ALU.is_gt) \
                   .then_inc(route_step, 1)
                dve.wait_ge(route_step, 8)
                dve.tensor_tensor(in_bin[:, :, :], above[:, 0:BINS, :], above[:, 1:BINS + 1, :], ALU.subtract) \
                   .then_inc(bins_done, 1)
                dve.tensor_copy(info[:, :, 1], mv[:, :, 0]).then_inc(route_step, 1)
                dve.tensor_copy(info[:, :, 2], rstd[:, :]).then_inc(route_step, 1)
                dve.wait_ge(counted, 2)
                dve.tensor_copy(upto[0][:, :, JT:], count_ps[:, 1, :].rearrange("p (k t) -> p k t", k=BINS)) \
                   .then_inc(route_step, 1)
                for i in range(5):
                    dve.wait_ge(route_step, 11 + i)
                    dve.tensor_tensor(upto[(i + 1) % 2][:, :, JT:], upto[i % 2][:, :, JT:],
                                      upto[i % 2][:, :, JT - (1 << i):2 * JT - (1 << i)], ALU.add) \
                       .then_inc(route_step, 1)
                sums = upto[1]
                dve.wait_ge(route_step, 16)
                dve.tensor_tensor(filled[:, :, :], sums[:, :, 2 * JT - 1:].to_broadcast([P, BINS, JT]),
                                  full_tiles.unsqueeze(1).to_broadcast([P, BINS, JT]), ALU.is_gt) \
                   .then_inc(route_step, 1)
                dve.wait_ge(route_step, 17)
                dve.tensor_reduce(ends[0][:, BINS:], filled[:, :, :], AX.X, ALU.add).then_inc(route_step, 1)
                for i in range(3):
                    dve.wait_ge(route_step, 18 + i)
                    dve.tensor_tensor(ends[(i + 1) % 2][:, BINS:], ends[i % 2][:, BINS:],
                                      ends[i % 2][:, BINS - (1 << i):2 * BINS - (1 << i)], ALU.add) \
                       .then_inc(route_step, 1)
                dve.wait_ge(route_step, 21)
                dve.tensor_scalar(starts[:, :], ends[1][:, BINS - 1:2 * BINS - 1], float(P), None, ALU.mult) \
                   .then_inc(route_step, 1)
                dve.tensor_tensor(place[:, :, :], count_ps[:, 0, :].rearrange("p (k t) -> p k t", k=BINS),
                                  sums[:, :, JT - 1:2 * JT - 1], ALU.add).then_inc(route_step, 1)
                dve.wait_ge(route_step, 23)
                dve.tensor_tensor(place[:, :, :], place[:, :, :], starts[:, :].unsqueeze(2).to_broadcast([P, BINS, JT]),
                                  ALU.add).then_inc(route_step, 1)
                dve.wait_ge(route_step, 24)
                dve.tensor_tensor(place[:, :, :], place[:, :, :], f32(in_bin[:, :, :]), ALU.mult).then_inc(route_step, 1)
                dve.wait_ge(route_step, 25)
                dve.tensor_reduce(slot_f[:, :], place[:, :, :].rearrange("p k t -> p t k"), AX.X, ALU.add) \
                   .then_inc(route_step, 1)
                dve.wait_ge(route_step, 26)
                dve.tensor_copy(slot[:, :], slot_f[:, :]).then_inc(route_step, 1)
                dve.wait_ge(route_step, 27)
                dve.tensor_scalar(lane[:, :], slot[:, :], P - 1, None, ALU.bitwise_and).then_inc(route_step, 1)
                dve.tensor_scalar(tile_of[:, :], slot[:, :], LOG_P, None, ALU.logical_shift_right).then_inc(route_step, 1)
                dve.wait_ge(route_step, 29)
                dve.scalar_tensor_tensor(out=row[:, :], in0=lane[:, :], scalar=float(TILES), in1=tile_of[:, :],
                                         op0=ALU.mult, op1=ALU.add).then_inc(route_step, 1)
                dve.tensor_tensor(passed_ends[:, :, :],
                                  tile_numbers.unsqueeze(2).to_broadcast([P, TILES, BINS - 1]),
                                  ends[1][:, BINS:2 * BINS - 1].unsqueeze(1).to_broadcast([P, TILES, BINS - 1]),
                                  ALU.is_ge).then_inc(route_step, 1)
                dve.wait_ge(route_step, 31)
                dve.tensor_reduce(tile_bin_f[:, :], passed_ends[:, :, :], AX.X, ALU.add).then_inc(route_step, 1)
                dve.wait_ge(route_step, 32)
                dve.tensor_copy(tile_bin[:, :], tile_bin_f[:, :]).then_inc(route_step, 1)

                for k in range(BINS):
                    low_w(k)

                def gather_rows(j, i):
                    dve.tensor_scalar(from_row[i][:, :], slots[:, bass.ds(j, 1), 0], T - 1.0, None, ALU.min) \
                       .then_inc(from_done, 1)

                def normalise(j, i):
                    dve.wait_ge(gathered[i], 16 * (j // RING + 1))
                    own_wait(dve, passed)
                    own = slots[:, bass.ds(j, 1), :]
                    dve.tensor_scalar(xf[i % 2][:, :], h1[i][:, :], own[:, :, 1], own[:, :, 2],
                                      ALU.subtract, ALU.mult).then_inc(xf_done, 1)

                def low(j, i):
                    dve.wait_ge(hi_done, j + 1)
                    dve.tensor_tensor(xf_lo[i % 2][:, :, :], turn_ps[i % 2][:, :].rearrange("p (c t) -> p c t", c=CC),
                                      f32(xf_hi[i % 2][:, :, :]), ALU.subtract).then_inc(lo_done, 1)

                def result(j, i, before):
                    if before or j >= RING:
                        dve.wait_ge(scattered[i], 16 * (j // RING))
                        own_wait(dve, passed)
                    dve.tensor_copy(to_row[i][:, :], slots[:, bass.ds(j, 1), 0])
                    dve.wait_ge(product_done, j + 1)
                    own_wait(dve, passed)
                    dve.tensor_tensor(res[i][:, :], bank[i % 2][:, :], h1[i][:, :], ALU.add).then_inc(res_done, 1)

                def one(j, i, before=False, after=False):
                    if after or j + RING - 1 < TILES:
                        gather_rows(j + RING - 1, (i - 1) % RING)
                    if before or j >= 1:
                        result(j - 1, (i - 1) % RING, before)
                    if after or j + 1 < TILES:
                        low(j + 1, (i + 1) % RING)
                    if after or j + 2 < TILES:
                        normalise(j + 2, (i + 2) % RING)

                dve.wait_ge(slots_loaded, 16)
                for j in range(RING - 1):
                    gather_rows(j, j)
                normalise(0, 0)
                normalise(1, 1)
                low(0, 0)
                all_tiles(dve, one)
                result(TILES - 1, RING - 1, True)


def metaformer_block(nc, x_t, w_qkv_t, rel_t, w_bins, ident, steps, tokens, tri, out):
    def dram(name, shape):
        return nc.dram_tensor(name, shape, F32, kind="Internal").ap()

    q_dram = dram("q_halves", [HEADS, P, 2, T])
    k_dram = dram("k_halves", [HEADS, P, 2, T])
    v_dram = dram("v_halves", [HEADS, P, 2, JT * DH])
    rel_dram = dram("rel_products", [HEADS, T, REL])
    h1_dram = dram("h1", [T, C])
    slots_dram = dram("slots", [TILES * P, 4])

    with ExitStack() as ctx:
        def sem(name):
            return ctx.enter_context(nc.semaphore(name))

        project(nc, sem, x_t, w_qkv_t, rel_t, ident, q_dram, k_dram, v_dram, rel_dram)
        stats = ctx.enter_context(nc.sbuf_tensor("h1_stats", [P, HEADS * JT, 6], F32))
        first = ctx.enter_context(nc.sbuf_tensor("h1_first", [P, HEADS * JT], F32))
        attend(nc, sem, q_dram, k_dram, v_dram, rel_dram, x_t, h1_dram, stats, first, ident)
        bin_experts(nc, sem, h1_dram, stats, first, w_bins, slots_dram, steps, tokens, tri, ident, out)


def kernel(x, L0_conv_w_qkv, L0_conv_rel_height, L0_conv_rel_width, L0_ffn_W):
    import numpy as np
    import concourse.bacc as bacc
    from concourse.bass_utils import run_bass_kernel_spmd

    x = np.asarray(x).reshape(C, T)
    rel = np.zeros((P, REL), np.float32)
    rel[:, :2 * SIDE - 1] = np.asarray(L0_conv_rel_width).T
    rel[:, P:P + 2 * SIDE - 1] = np.asarray(L0_conv_rel_height).T
    tokens = np.zeros((P, JT, 4), np.float32)
    tokens[:, :, 0] = np.arange(T).reshape(JT, P).T
    arrays = {
        "x_t": np.ascontiguousarray(x.T),
        "w_qkv_t": np.ascontiguousarray(np.asarray(L0_conv_w_qkv).T),
        "rel_t": rel,
        "w_bins": np.ascontiguousarray(np.asarray(L0_ffn_W)),
        "ident": np.eye(P, dtype=np.float32),
        "steps": np.tile(np.concatenate([THRESHOLDS, np.arange(JT) * P, np.arange(TILES)]).astype(np.float32), (P, 1)),
        "tokens": tokens,
        "tri": np.concatenate([np.triu(np.ones((P, P), np.float32), 1), np.ones((P, P), np.float32)], axis=1),
    }
    nc = bacc.Bacc("TRN2", target_bir_lowering=False, num_devices=1)
    ins = [nc.dram_tensor(name, a.shape, F32, kind="ExternalInput").ap() for name, a in arrays.items()]
    out = nc.dram_tensor("out", (T, C), F32, kind="ExternalOutput").ap()
    metaformer_block(nc, *ins, out)
    result = run_bass_kernel_spmd(nc, [arrays], core_ids=[0]).results[0]["out"]
    return np.ascontiguousarray(result.T).reshape(1, C, SIDE, SIDE)
```

```python
from contextlib import ExitStack

import concourse.bass as bass
from concourse import mybir
from concourse.alu_op_type import AluOpType as ALU

P = 128
C = 512
CC = C // P
SIDE = 64
T = SIDE * SIDE
HEADS = 4
DH = C // HEADS
B = 512
NB = T // B
TPB = B // P
JT = T // P
BINS = 8
THRESHOLDS = [-1.5, -1.0, -0.5, 0.0, 0.5, 1.0, 1.5]
SCALE = DH ** -0.5
EPS_C = 1e-6
EPS_T = 1e-5
CH = 1024
CPT = T // CH
TILES = JT + BINS
LOG_P = P.bit_length() - 1
NORMED, PLACED, ROUTED = 6, 30, 34
REL = 2 * P

F32 = mybir.dt.float32
F32R = mybir.dt.float32r
I32 = mybir.dt.int32
ACT = mybir.ActivationFunctionType
AX = mybir.AxisListType


def f32(ap):
    return ap.bitcast(F32)


def own_wait(eng, passed):
    eng.sem_inc(passed, 1)


def split_product(pe, out, w_hi, w_lo, m_hi, m_lo, first, last):
    pe.matmul(out, w_lo, m_hi, start=first, stop=False)
    pe.matmul(out, w_hi, m_lo, start=False, stop=False)
    return pe.matmul(out, w_hi, m_hi, start=False, stop=last)


def load_k_chunk(sp, k_dram, k_sb, h, c, loaded):
    keys = slice(c * CH, (c + 1) * CH)
    sp.dma_start(f32(k_sb[:, :, keys]), k_dram[h, :, :, keys]).then_inc(loaded, 16)


def load_q_tile(sp, q_dram, q_sb, h, b, t, loaded):
    sp.dma_start(f32(q_sb[:, :, t * P:(t + 1) * P]), q_dram[h, :, :, bass.ds(b * B + t * P, P)]).then_inc(loaded, 16)


def load_block_bias(sp, rel_dram, lw, lh, h, b, loaded):
    for xx in range(P // SIDE):
        own = slice(xx * SIDE, (xx + 1) * SIDE)
        src = rel_dram[h, bass.ds(b * B, B), :].rearrange("(k x y) r -> x y k r", x=P // SIDE, y=SIDE)[xx]
        by_column = bass.AP(src.tensor, src.offset + (SIDE - 1), [[REL - 1, SIDE], [P * REL, TPB], [1, SIDE]])
        sp.dma_start(lw[own, :, :], by_column).then_inc(loaded, 16)
        by_row = bass.AP(src.tensor, src.offset + (P + SIDE - 1 - xx) - b * (B // SIDE),
                         [[REL, SIDE], [P * REL - P // SIDE, TPB], [1, SIDE]])
        sp.dma_start(lh[own, :, :], by_row).then_inc(loaded, 16)


def project(nc, sem, x_t, w_qkv_t, rel_t, ident_in, ident, q_dram, k_dram, v_dram, rel_dram, k_sb, q_sb, lw, lh,
            k_loaded, q_loaded, bias_loaded):
    OUTS = 3 * HEADS
    RING = 4
    PER = OUTS // RING
    NORM = 2 * TPB + 5 + TPB

    with ExitStack() as ctx:
        def sb(name, shape, dt=F32):
            return ctx.enter_context(nc.sbuf_tensor(name, shape, dt))

        def ps(name, cols=B):
            return ctx.enter_context(nc.psum_tensor(name, [P, cols], F32))

        w_raw = [sb(f"p_w_raw{i}", [P, CC, C]) for i in range(3)]
        w_hi = [sb(f"p_w_hi{i}", [P, CC, C], F32R) for i in range(3)]
        w_lo = [sb(f"p_w_lo{i}", [P, CC, C], F32R) for i in range(3)]
        rel_raw = sb("p_rel_raw", [P, REL])
        rel_hi = sb("p_rel_hi", [P, REL], F32R)
        rel_lo = sb("p_rel_lo", [P, REL], F32R)
        eps = sb("p_eps", [P, 1])
        warm = sb("p_warm", [P, 1])
        x_in = [sb(f"p_x{i}", [P, TPB, C]) for i in range(2)]
        xn = sb("p_xn", [P, TPB, C])
        stats = sb("p_stats", [P, TPB, 6])
        mv = sb("p_mv", [P, TPB, 2])
        dev = sb("p_dev", [P, TPB])
        rstd = sb("p_rstd", [P, TPB])
        newton = sb("p_newton", [P, TPB])
        x_hi = [sb(f"p_xhi{i}", [P, CC, B], F32R) for i in range(2)]
        x_lo = [sb(f"p_xlo{i}", [P, CC, B], F32R) for i in range(2)]
        q_f = [sb(f"p_qf{i}", [P, B]) for i in range(2)]
        outs = [sb(f"p_out{i}", [P, 2, B], F32R) for i in range(RING)]
        rel = [sb(f"p_rel{i}", [P, TPB, REL]) for i in range(2)]

        bank = [ps(f"p_bank{i}") for i in range(RING)]
        turn_ps = [ps(f"p_turn{i}") for i in range(2)]
        rel_ps = ps("p_relps", TPB * REL)

        passed = sem("p_passed")
        w_loaded = [sem(f"p_w_loaded{i}") for i in range(3)]
        small_loaded = sem("p_small_loaded")
        w_hi_done = sem("p_w_hi_done")
        w_lo_done = sem("p_w_lo_done")
        rel_hi_done = sem("p_rel_hi_done")
        rel_lo_done = sem("p_rel_lo_done")
        eps_done = sem("p_eps_done")
        x_loaded = [sem(f"p_x_loaded{i}") for i in range(2)]
        norm_step = sem("p_norm_step")
        dev_done = sem("p_dev_done")
        turned = sem("p_turned")
        x_hi_done = sem("p_x_hi_done")
        x_lo_done = sem("p_x_lo_done")
        product_done = sem("p_product_done")
        out_stored = [sem(f"p_out_stored{i}") for i in range(RING)]
        hi_done = sem("p_hi_done")
        lo_done = sem("p_lo_done")
        rel_done = sem("p_rel_done")
        rel_copied = sem("p_rel_copied")
        rel_stored = [sem(f"p_rel_stored{i}") for i in range(2)]

        with nc.Block() as block:

            def all_blocks(eng, one):
                with eng.Fori(0, NB // 2 - 1) as m:
                    one(m * 2, 0, True, True)
                    one(m * 2 + 1, 1, True, True)
                one(NB - 2, 0, True, False)
                one(NB - 1, 1, False, False)

            @block.sync
            def _(sp):
                sp.sem_inc(lo_done, RING)
                sp.sem_inc(x_lo_done, 2)
                sp.sem_inc(rel_copied, 1)
                for i in range(RING):
                    sp.sem_inc(out_stored[i], 32)
                for i in range(2):
                    sp.sem_inc(rel_stored[i], 16)

                def load_x(tb, p):
                    sp.dma_start(x_in[p][:, :, :], x_t[bass.ds(tb * B, B), :].rearrange("(t p) c -> p t c", p=P)) \
                      .then_inc(x_loaded[p], 16)

                load_x(0, 0)
                sp.dma_start(ident[:, :], ident_in).then_inc(small_loaded, 16)
                sp.dma_start(rel_raw[:, :], rel_t).then_inc(small_loaded, 16)
                for i in range(3):
                    sp.dma_start(w_raw[i][:, :, :], w_qkv_t[:, i * C:(i + 1) * C].rearrange("(c p) o -> p c o", p=P)) \
                      .then_inc(w_loaded[i], 16)
                load_x(1, 1)

                def store_out(tb, idx):
                    r = idx % RING
                    sp.wait_ge(lo_done, tb * OUTS + idx + 1 + RING)
                    own_wait(sp, passed)
                    cols = bass.ds(tb * B, B)
                    for half in range(2):
                        src = f32(outs[r][:, half, :])
                        if idx < HEADS:
                            dst = q_dram[idx, :, half, cols]
                        elif idx < 2 * HEADS:
                            dst = k_dram[idx - HEADS, :, half, cols]
                        else:
                            jt = tb * TPB + idx - 2 * HEADS
                            dst = v_dram[:, :, half, bass.ds(jt * DH, DH)].rearrange("h p d -> p h d")
                            src = src.rearrange("p (h d) -> p h d", h=HEADS)
                        sp.dma_start(dst, src).then_inc(out_stored[r], 16)

                def store_rel(tb, h):
                    i = h % 2
                    sp.wait_ge(rel_copied, tb * HEADS + h + 1 + 1)
                    own_wait(sp, passed)
                    dst = rel_dram[h, bass.ds(tb * B, B), :].rearrange("(k p) r -> p k r", p=P)
                    sp.dma_start(dst, rel[i][:, :, :]).then_inc(rel_stored[i], 16)

                def load_ahead(tb, part):
                    assert (CPT - 1) * CH <= (NB - 1) * B
                    if part == 0:
                        for i in range(RING):
                            sp.wait_ge(out_stored[i], 32 * (tb * PER + 1))
                        for i in range(2):
                            sp.wait_ge(rel_stored[i], 16 * (tb * HEADS // 2 + 1))
                        for t in range(TPB):
                            load_q_tile(sp, q_dram, q_sb, 0, 0, t, q_loaded[t])
                        load_block_bias(sp, rel_dram, lw, lh, 0, 0, bias_loaded)
                    elif part < CPT:
                        load_k_chunk(sp, k_dram, k_sb, 0, part - 1, k_loaded[part - 1])

                def one(tb, p, more, more2):
                    for idx in range(OUTS):
                        store_out(tb, idx)
                        if 1 <= idx <= HEADS:
                            store_rel(tb, idx - 1)
                        if not more and idx >= HEADS - 1 and (idx - HEADS + 1) % 2 == 0:
                            load_ahead(tb, (idx - HEADS + 1) // 2)
                    if more2:
                        sp.wait_ge(norm_step, (tb + 1) * NORM)
                        own_wait(sp, passed)
                        load_x(tb + 2, p)

                all_blocks(sp, one)
                for i in range(RING):
                    sp.wait_ge(out_stored[i], 32 * (NB * PER + 1))
                for i in range(2):
                    sp.wait_ge(rel_stored[i], 16 * (NB * HEADS // 2 + 1))

            @block.gpsimd
            def _(pool):
                pool.memset(eps[:, :], EPS_C).then_inc(eps_done, 1)

            @block.tensor
            def _(pe):
                def turn(tb, t):
                    pe.wait_ge(norm_step, tb * NORM + NORM - TPB + t + 1)
                    pe.wait_ge(x_lo_done, tb * TPB + t + 1)
                    for c in range(CC):
                        mm = pe.transpose(turn_ps[t % 2][:, c * P:(c + 1) * P], xn[:, t, c * P:(c + 1) * P], ident[:, :])
                    mm.then_inc(turned, 1)

                def product(tb, p, idx):
                    r = idx % RING
                    pe.wait_ge(lo_done, tb * OUTS + idx + 1)
                    part, o = divmod(idx, HEADS)
                    own = slice(o * P, (o + 1) * P)
                    for c in range(CC):
                        if part < 2:
                            w, m = (w_hi[part][:, c, own], w_lo[part][:, c, own]), (x_hi[p][:, c, :], x_lo[p][:, c, :])
                        else:
                            w, m = (x_hi[p][:, c, own], x_lo[p][:, c, own]), (w_hi[2][:, c, :], w_lo[2][:, c, :])
                        mm = split_product(pe, bank[r][:, :], *w, *m, c == 0, c == CC - 1)
                    mm.then_inc(product_done, 1)

                def relative(tb, h):
                    pe.wait_ge(lo_done, tb * OUTS + h + 1 + RING)
                    pe.wait_ge(rel_copied, tb * HEADS + h + 1)
                    for k in range(TPB):
                        t = slice(k * P, (k + 1) * P)
                        mm = split_product(pe, rel_ps[:, k * REL:(k + 1) * REL], outs[h][:, 0, t], outs[h][:, 1, t],
                                           rel_hi[:, :], rel_lo[:, :], True, True)
                    mm.then_inc(rel_done, 1)

                def one(tb, p, more, more2):
                    pe.wait_ge(x_lo_done, (tb + 1) * TPB + 2)
                    for idx in range(OUTS):
                        if idx % HEADS == 0:
                            pe.wait_ge(w_lo_done, 1 + idx // HEADS)
                        if idx == 1:
                            pe.wait_ge(rel_lo_done, 1)
                        product(tb, p, idx)
                        if 1 <= idx <= HEADS:
                            relative(tb, idx - 1)
                        if more and idx >= OUTS - 1 - TPB and idx < OUTS - 1:
                            turn(tb + 1, idx - (OUTS - 1 - TPB))

                pe.wait_ge(small_loaded, 32)
                for t in range(TPB):
                    turn(0, t)
                all_blocks(pe, one)

            @block.scalar
            def _(act):
                def deviation(tb):
                    act.wait_ge(norm_step, tb * NORM + 2 * TPB)
                    act.activation(dev[:, :], mv[:, :, 1], ACT.Sqrt, bias=eps[:, 0:1]).then_inc(dev_done, 1)

                def norm_high(tb, p, t):
                    act.wait_ge(turned, tb * TPB + t + 1)
                    act.activation(x_hi[p][:, :, t * P:(t + 1) * P],
                                   turn_ps[t % 2][:, :].rearrange("p (c t) -> p c t", c=CC), ACT.Copy) \
                       .then_inc(x_hi_done, 1)

                def high(tb, idx):
                    r = idx % RING
                    act.wait_ge(product_done, tb * OUTS + idx + 1)
                    act.wait_ge(out_stored[r], (tb * PER + idx // RING + 1) * 32)
                    if idx < HEADS:
                        if idx >= 2:
                            act.wait_ge(lo_done, tb * OUTS + idx + 1 - 2 + RING)
                        act.activation(q_f[idx % 2][:, :], bank[r][:, :], ACT.Copy, scale=SCALE)
                        act.activation(outs[r][:, 0, :], bank[r][:, :], ACT.Copy, scale=SCALE).then_inc(hi_done, 1)
                    else:
                        if idx < 2 * HEADS:
                            act.wait_ge(rel_done, tb * HEADS + idx - HEADS + 1)
                        act.activation(outs[r][:, 0, :], bank[r][:, :], ACT.Copy).then_inc(hi_done, 1)

                def relative(tb, h):
                    i = h % 2
                    act.wait_ge(rel_done, tb * HEADS + h + 1)
                    act.wait_ge(rel_stored[i], (tb * (HEADS // 2) + h // 2 + 1) * 16)
                    act.activation(rel[i][:, :, :], rel_ps[:, :].rearrange("p (k r) -> p k r", k=TPB), ACT.Copy) \
                       .then_inc(rel_copied, 1)

                def one(tb, p, more, more2):
                    for idx in range(OUTS):
                        high(tb, idx)
                        if 1 <= idx <= HEADS:
                            relative(tb, idx - 1)
                        if more and idx == HEADS + 1:
                            deviation(tb + 1)
                        if more and idx >= OUTS - 1 - TPB and idx < OUTS - 1:
                            norm_high(tb + 1, 1 - p, idx - (OUTS - 1 - TPB))

                def high_w(i):
                    act.wait_ge(w_loaded[i], 16)
                    act.activation(w_hi[i][:, :, :], w_raw[i][:, :, :], ACT.Copy).then_inc(w_hi_done, 1)

                act.wait_ge(eps_done, 1)
                act.activation(warm[:, :], eps[:, :], ACT.Sqrt)
                deviation(0)
                high_w(0)
                act.wait_ge(small_loaded, 32)
                act.activation(rel_hi[:, :], rel_raw[:, :], ACT.Copy).then_inc(rel_hi_done, 1)
                for t in range(TPB):
                    norm_high(0, 0, t)
                high_w(1)
                high_w(2)
                all_blocks(act, one)

            @block.vector
            def _(dve):
                def statistics(tb, p):
                    n = tb * NORM
                    dve.wait_ge(x_loaded[p], 16 * (tb // 2 + 1))
                    for t in range(TPB):
                        dve.bn_stats(stats[:, t, :], x_in[p][:, t, :]).then_inc(norm_step, 1)
                    for t in range(TPB):
                        dve.wait_ge(norm_step, n + TPB + t)
                        own_wait(dve, passed)
                        dve.bn_aggr(mv[:, t, :], stats[:, t, :]).then_inc(norm_step, 1)

                def normalise(tb, p):
                    n = tb * NORM + 2 * TPB
                    dve.wait_ge(dev_done, tb + 1)
                    dve.reciprocal(rstd[:, :], dev[:, :]).then_inc(norm_step, 1)
                    dve.wait_ge(norm_step, n + 1)
                    dve.tensor_tensor(newton[:, :], rstd[:, :], rstd[:, :], ALU.mult).then_inc(norm_step, 1)
                    dve.wait_ge(norm_step, n + 2)
                    dve.scalar_tensor_tensor(out=newton[:, :], in0=mv[:, :, 1], scalar=EPS_C, in1=newton[:, :],
                                             op0=ALU.add, op1=ALU.mult).then_inc(norm_step, 1)
                    dve.wait_ge(norm_step, n + 3)
                    dve.tensor_scalar(newton[:, :], newton[:, :], -0.5, 1.5, ALU.mult, ALU.add).then_inc(norm_step, 1)
                    dve.wait_ge(norm_step, n + 4)
                    dve.tensor_tensor(rstd[:, :], rstd[:, :], newton[:, :], ALU.mult).then_inc(norm_step, 1)
                    dve.wait_ge(norm_step, n + 5)
                    for t in range(TPB):
                        dve.tensor_scalar(xn[:, t, :], x_in[p][:, t, :], mv[:, t, 0:1], rstd[:, t:t + 1],
                                          ALU.subtract, ALU.mult).then_inc(norm_step, 1)

                def norm_low(tb, p, t):
                    dve.wait_ge(x_hi_done, tb * TPB + t + 1)
                    own = x_lo[p][:, :, t * P:(t + 1) * P], x_hi[p][:, :, t * P:(t + 1) * P]
                    dve.tensor_tensor(own[0], turn_ps[t % 2][:, :].rearrange("p (c t) -> p c t", c=CC), f32(own[1]),
                                      ALU.subtract).then_inc(x_lo_done, 1)

                def low(tb, idx):
                    r = idx % RING
                    dve.wait_ge(hi_done, tb * OUTS + idx + 1)
                    whole = q_f[idx % 2] if idx < HEADS else bank[r]
                    dve.tensor_tensor(outs[r][:, 1, :], whole[:, :], f32(outs[r][:, 0, :]), ALU.subtract) \
                       .then_inc(lo_done, 1)

                def one(tb, p, more, more2):
                    for idx in range(OUTS):
                        low(tb, idx)
                        if more and idx == HEADS - 1:
                            statistics(tb + 1, 1 - p)
                        if more and idx == HEADS + 2:
                            normalise(tb + 1, 1 - p)
                        if more and idx >= OUTS - 1 - TPB and idx < OUTS - 1:
                            norm_low(tb + 1, 1 - p, idx - (OUTS - 1 - TPB))

                def low_w(i):
                    dve.wait_ge(w_hi_done, i + 1)
                    dve.tensor_tensor(w_lo[i][:, :, :], w_raw[i][:, :, :], f32(w_hi[i][:, :, :]), ALU.subtract) \
                       .then_inc(w_lo_done, 1)

                statistics(0, 0)
                normalise(0, 0)
                low_w(0)
                dve.wait_ge(rel_hi_done, 1)
                dve.tensor_tensor(rel_lo[:, :], rel_raw[:, :], f32(rel_hi[:, :]), ALU.subtract).then_inc(rel_lo_done, 1)
                for t in range(TPB):
                    norm_low(0, 0, t)
                low_w(1)
                low_w(2)
                all_blocks(dve, one)


def merge_heads(dve, stats, mv, t, done):
    dve.bn_aggr(mv[:, t, :], stats[:, :, :].rearrange("p (h t) s -> p t h s", h=HEADS)[:, t, :, :]).then_inc(done, 1)


def attend(nc, sem, q_dram, k_dram, v_dram, rel_dram, x_t, h1_dram, stats, first, mv, ident, k_sb, q_sb,
           lw, lh, k_loaded, q_loaded, bias_loaded):
    NBLK = HEADS * NB
    STEPS = TPB * CPT
    JPC = CH // P
    POS = 4
    BANKS = 3
    AHEAD = BANKS - 1
    QUOTA = [0, 0, 0] + [4] * 7 + [2, 1, 1]
    FIRST = [sum(QUOTA[:s]) for s in range(len(QUOTA))]
    assert sum(QUOTA) == JT
    assert all(FIRST[2 * CPT + c] + AHEAD >= (c + 1) * JPC for c in range(CPT))
    START = 3
    OUT = len(QUOTA)

    with ExitStack() as ctx:
        def sb(name, shape, dt=F32):
            return ctx.enter_context(nc.sbuf_tensor(name, shape, dt))

        v_sb = sb("a_v", [P, 2, T], F32R)
        rows01 = [[sb(f"a_rows{par}{t}", [P, T]) for t in range(2)] for par in range(2)]
        rows23 = [sb(f"a_rows{t}", [P, T]) for t in range(2, TPB)]
        lw = [lw, sb("a_lw1", [P, TPB, SIDE])]
        lh = [lh, sb("a_lh1", [P, TPB, SIDE])]
        pos = [sb(f"a_pos{i}", [P, CH]) for i in range(POS)]
        p_hi = [sb(f"a_phi{i}", [P, B], F32R) for i in range(BANKS)]
        p_lo = [sb(f"a_plo{i}", [P, B], F32R) for i in range(BANKS)]
        tops = sb("a_tops", [P, TPB, CPT])
        neg_top = sb("a_neg_top", [P, TPB])
        sums = [sb(f"a_sums{i}", [P, TPB, CPT]) for i in range(2)]
        total = sb("a_total", [P, TPB])
        inv = sb("a_inv", [P, TPB])
        o_t = sb("a_o_t", [P, B])
        x_own = sb("a_x_own", [P, TPB, DH])
        o_out = sb("a_o_out", [P, TPB, DH])

        score_ps = [ctx.enter_context(nc.psum_tensor(f"a_score{i}", [P, CH], F32)) for i in range(2)]
        pt_ps = [ctx.enter_context(nc.psum_tensor(f"a_pt{i}", [P, B], F32)) for i in range(BANKS)]
        o_ps = ctx.enter_context(nc.psum_tensor("a_o", [P, B], F32))
        turn_ps = pt_ps[0]

        passed = sem("a_passed")
        bias_loaded = [bias_loaded, sem("a_bias_loaded1")]
        x_loaded = sem("a_x_loaded")
        v_loaded = [sem(f"a_v_loaded{i}") for i in range(CPT)]
        scored = sem("a_scored")
        pos_done = sem("a_pos_done")
        biased = sem("a_biased")
        neg_done = sem("a_neg_done")
        exp_done = sem("a_exp_done")
        turned = sem("a_turned")
        hi_done = sem("a_hi_done")
        lo_done = sem("a_lo_done")
        weighed = sem("a_weighed")
        o_copied = sem("a_o_copied")
        o_turned = sem("a_o_turned")
        total_done = sem("a_total_done")
        inv_done = sem("a_inv_done")
        scaled = sem("a_scaled")
        o_done = sem("a_o_done")
        merged = sem("a_merged")
        seen = sem("a_seen")
        stored = sem("a_stored")

        def rows(par, t):
            return rows01[par][t] if t < 2 else rows23[t - 2]

        def all_blocks(eng, one, tail):
            one(0, 0, 0)
            one(1, 1, 1)
            with eng.Fori(1, NBLK // 2) as m:
                one(m * 2, 0, 2)
                one(m * 2 + 1, 1, 2)
            tail(NBLK - 1, 1)

        with nc.Block() as block:

            @block.sync
            def _(sp):
                sp.sem_inc(biased, POS)
                sp.sem_inc(o_copied, 1)
                sp.sem_inc(o_turned, 1)
                sp.sem_inc(scaled, 1)
                sp.sem_inc(o_done, 1)
                sp.sem_inc(stored, 16)

                def load_k(h, chunks, wait=True):
                    for c in chunks:
                        if wait:
                            sp.wait_ge(scored, h * NB * STEPS - CPT + c + 1)
                            own_wait(sp, passed)
                        load_k_chunk(sp, k_dram, k_sb, h, c, k_loaded[c])

                def load_v(h, chunks, wait=True):
                    for c in chunks:
                        if wait:
                            sp.wait_ge(weighed, (h * NB - 1) * JT + (c + 1) * JPC)
                            own_wait(sp, passed)
                        sp.dma_start(f32(v_sb[:, :, c * CH:(c + 1) * CH]), v_dram[h, :, :, c * CH:(c + 1) * CH]) \
                          .then_inc(v_loaded[c], 16)

                def load_q(h, b, tiles, wait=True):
                    for t in tiles:
                        if wait:
                            sp.wait_ge(scored, (h * NB + b - 1) * STEPS + (t + 1) * CPT)
                            own_wait(sp, passed)
                        load_q_tile(sp, q_dram, q_sb, h, b, t, q_loaded[t])

                def load_bias(h, b, par, wait=True):
                    if wait:
                        sp.wait_ge(biased, (h * NB + b - 1) * STEPS + POS)
                        own_wait(sp, passed)
                    load_block_bias(sp, rel_dram, lw[par], lh[par], h, b, bias_loaded[par])

                def place(dram, h, b):
                    return dram[bass.ds(b * B, B), bass.ds(h * DH, DH)].rearrange("(k p) d -> p k d", p=P)

                def store_out(h, b):
                    sp.wait_ge(o_done, h * NB + b + 1 + 1)
                    own_wait(sp, passed)
                    sp.dma_start(place(h1_dram, h, b), o_out[:, :, :]).then_inc(stored, 16)

                def load_x(h, b):
                    sp.dma_start(x_own[:, :, :], place(x_t, h, b)).then_inc(x_loaded, 16)

                load_k(0, [CPT - 1], False)
                load_bias(0, 1, 1, False)
                load_v(0, range(CPT), False)
                load_x(0, 0)
                load_q(0, 1, range(TPB))

                def around(h, b, par, out, x):
                    load_bias(h, b, par)
                    load_q(h, b, [0])
                    store_out(*out)
                    load_x(*x)
                    load_q(h, b, range(1, TPB))

                def rest_of_head(h):
                    around(h, 3, 1, (h, 0), (h, 1))
                    with sp.Fori(2, NB // 2) as i:
                        for u in range(2):
                            b = i * 2 + u
                            around(h, b, u, (h, b - 3), (h, b - 2))

                load_bias(0, 2, 0)
                load_q(0, 2, range(TPB))
                rest_of_head(0)
                with sp.Fori(1, HEADS) as h:
                    load_bias(h, 0, 0)
                    load_q(h, 0, [0])
                    store_out(h - 1, NB - 3)
                    load_x(h - 1, NB - 2)
                    load_q(h, 0, [1, 2])
                    load_k(h, range(CPT - 1))
                    load_q(h, 0, [TPB - 1])
                    load_k(h, [CPT - 1])
                    load_bias(h, 1, 1)
                    load_q(h, 1, [0])
                    store_out(h - 1, NB - 2)
                    load_x(h - 1, NB - 1)
                    load_v(h, [0])
                    load_q(h, 1, [1])
                    load_v(h, range(1, CPT))
                    load_q(h, 1, [2, 3])
                    around(h, 2, 0, (h - 1, NB - 1), (h, 0))
                    rest_of_head(h)
                for b in range(NB - 3, NB):
                    store_out(HEADS - 1, b)
                    if b + 1 < NB:
                        load_x(HEADS - 1, b + 1)
                sp.wait_ge(stored, (NBLK + 1) * 16)

            @block.gpsimd
            def _(pool):
                def positions(n, par):
                    for s in range(STEPS):
                        t, c = divmod(s, CPT)
                        if s == 0:
                            pool.wait_ge(bias_loaded[par], 64 * (n // 2 + 1))
                        pool.wait_ge(biased, n * STEPS + s + 1)
                        own_wait(pool, passed)
                        rows_of = slice(c * (CH // SIDE), (c + 1) * (CH // SIDE))
                        pool.tensor_tensor(
                            pos[s % POS][:, :].rearrange("p (x y) -> p x y", y=SIDE),
                            lw[par][:, t, :].unsqueeze(1).to_broadcast([P, CH // SIDE, SIDE]),
                            lh[par][:, t, rows_of].unsqueeze(2).to_broadcast([P, CH // SIDE, SIDE]),
                            ALU.add).then_inc(pos_done, 1)

                with pool.Fori(0, NBLK // 2) as m:
                    for par in range(2):
                        positions(m * 2 + par, par)

            @block.tensor
            def _(pe):
                def score(n, par, s):
                    t, c = divmod(s, CPT)
                    if c == 0:
                        pe.wait_ge(q_loaded[t], 16 * (n + 1))
                    if t == 0:
                        pe.wait_ge(k_loaded[c], 16 * (n // NB + 1))
                    pe.wait_ge(biased, n * STEPS + s - 1 + POS)
                    q = slice(t * P, (t + 1) * P)
                    for half in range(CH // B):
                        k = slice(c * CH + half * B, c * CH + (half + 1) * B)
                        out = score_ps[s % 2][:, half * B:(half + 1) * B]
                        mm = split_product(pe, out, q_sb[:, 0, q], q_sb[:, 1, q],
                                           k_sb[:, 0, k], k_sb[:, 1, k], True, True)
                    mm.then_inc(scored, 1)

                def turn(n, par, j):
                    g = n * JT + j
                    if j % JPC == 0:
                        pe.wait_ge(exp_done, n * STEPS + STEPS - CPT + j // JPC + 1)
                    if j == 0:
                        pe.wait_ge(scaled, n + 1)
                    if j >= BANKS:
                        pe.wait_ge(lo_done, g - BANKS + 1)
                    for t in range(TPB):
                        mm = pe.transpose(pt_ps[j % BANKS][:, t * P:(t + 1) * P], rows(par, t)[:, j * P:(j + 1) * P],
                                          ident[:, :])
                    mm.then_inc(turned, 1)

                def weigh(n, j):
                    g = n * JT + j
                    if j == 0:
                        pe.wait_ge(o_copied, n + 1)
                    if j % JPC == 0:
                        pe.wait_ge(v_loaded[j // JPC], 16 * (n // NB + 1))
                    pe.wait_ge(lo_done, g + 1)
                    split_product(pe, o_ps[:, :], v_sb[:, 0, j * P:(j + 1) * P], v_sb[:, 1, j * P:(j + 1) * P],
                                  p_hi[j % BANKS][:, :], p_lo[j % BANKS][:, :], j == 0, j == JT - 1).then_inc(weighed, 1)

                def turn_out(n):
                    pe.wait_ge(o_copied, n + 1 + 1)
                    for t in range(TPB):
                        mm = pe.transpose(turn_ps[:, t * P:(t + 1) * P], o_t[:, t * P:(t + 1) * P], ident[:, :])
                    mm.then_inc(o_turned, 1)

                def values(n, par, s):
                    if 0 <= s - (START - AHEAD) < AHEAD:
                        turn(n, par, s - (START - AHEAD))
                    for j in range(FIRST[s], FIRST[s] + QUOTA[s]):
                        if j + AHEAD < JT:
                            turn(n, par, j + AHEAD)
                        weigh(n, j)

                def one(n, par, before):
                    for s in range(STEPS):
                        score(n, par, s)
                        if before and s < OUT:
                            values(n - 1, 1 - par, s)
                        if before and s == OUT:
                            turn_out(n - 1)

                def tail(n, par):
                    for s in range(OUT):
                        values(n, par, s)
                    turn_out(n)

                all_blocks(pe, one, tail)

            @block.scalar
            def _(act):
                def exponent(n, par, t, c):
                    if c == 0:
                        act.wait_ge(neg_done, n * TPB + t + 1)
                    row = rows(par, t)[:, c * CH:(c + 1) * CH]
                    act.activation(row, row, ACT.Exp, bias=neg_top[:, t:t + 1],
                                   accum_out=sums[par][:, t, c:c + 1]).then_inc(exp_done, 1)

                def high(n, j):
                    g = n * JT + j
                    act.wait_ge(turned, g + 1)
                    if j >= BANKS:
                        act.wait_ge(weighed, g - BANKS + 1)
                    act.activation(p_hi[j % BANKS][:, :], pt_ps[j % BANKS][:, :], ACT.Copy).then_inc(hi_done, 1)

                def copy_out(n):
                    act.wait_ge(weighed, (n + 1) * JT)
                    act.wait_ge(o_done, n + 1)
                    act.activation(o_t[:, :], o_ps[:, :], ACT.Copy).then_inc(o_copied, 1)

                def scale_out(n):
                    act.wait_ge(inv_done, n + 1)
                    act.wait_ge(o_turned, n + 1 + 1)
                    for t in range(TPB):
                        own = slice(t * P, (t + 1) * P)
                        ins = act.activation(o_t[:, own], turn_ps[:, own], ACT.Copy, scale=inv[:, t:t + 1])
                    ins.then_inc(scaled, 1)

                def highs(n, s):
                    if s == START - 1:
                        for j in range(AHEAD):
                            high(n, j)
                    for j in range(FIRST[s], FIRST[s] + QUOTA[s]):
                        if j + AHEAD < JT:
                            high(n, j + AHEAD)

                def last_tile(n, par, s):
                    chunks = {-1: [0, 1], START: [2], START + 1: [3]}.get(s, [])
                    for c in chunks:
                        exponent(n, par, TPB - 1, c)

                def one(n, par, before):
                    for s in range(-1, STEPS):
                        if before and s < OUT:
                            if s >= 0:
                                highs(n - 1, s)
                            last_tile(n - 1, 1 - par, s)
                        if before and s == OUT:
                            copy_out(n - 1)
                        if s >= CPT:
                            exponent(n, par, s // CPT - 1, s % CPT)
                        if before and s == STEPS - 1:
                            scale_out(n - 1)

                def tail(n, par):
                    for s in range(-1, OUT):
                        if s >= 0:
                            highs(n, s)
                        last_tile(n, par, s)
                    copy_out(n)
                    scale_out(n)

                all_blocks(act, one, tail)

            @block.vector
            def _(dve):
                def bias(n, par, s):
                    t, c = divmod(s, CPT)
                    dve.wait_ge(pos_done, n * STEPS + s + 1)
                    dve.wait_ge(scored, n * STEPS + s + 1)
                    own_wait(dve, passed)
                    dve.tensor_tensor_reduce(
                        rows(par, t)[:, c * CH:(c + 1) * CH], score_ps[s % 2][:, :], pos[s % POS][:, :],
                        1.0, -3.0e38, ALU.add, ALU.max, tops[:, t, c:c + 1]).then_inc(biased, 1)

                def maximum(n, t):
                    dve.wait_ge(biased, n * STEPS + (t + 1) * CPT + POS)
                    dve.tensor_reduce(neg_top[:, t:t + 1], tops[:, t, :], AX.X, ALU.max, negate=True).then_inc(neg_done, 1)

                def low(n, j):
                    g = n * JT + j
                    dve.wait_ge(hi_done, g + 1)
                    dve.tensor_tensor(p_lo[j % BANKS][:, :], pt_ps[j % BANKS][:, :], f32(p_hi[j % BANKS][:, :]), ALU.subtract) \
                       .then_inc(lo_done, 1)

                def lows(n, s):
                    if s == START - 1:
                        for j in range(AHEAD):
                            low(n, j)
                    for j in range(FIRST[s], FIRST[s] + QUOTA[s]):
                        if j + AHEAD < JT:
                            low(n, j + AHEAD)

                def denominators(n, par):
                    dve.wait_ge(exp_done, (n + 1) * STEPS)
                    dve.tensor_reduce(total[:, :], sums[par][:, :, :], AX.X, ALU.add).then_inc(total_done, 1)
                    dve.wait_ge(total_done, n + 1)
                    dve.reciprocal(inv[:, :], total[:, :]).then_inc(inv_done, 1)

                def add_input(n):
                    dve.wait_ge(scaled, n + 1 + 1)
                    dve.wait_ge(x_loaded, 16 * (n + 1))
                    dve.wait_ge(stored, 16 * (n + 1))
                    dve.tensor_tensor(o_out[:, :, :], o_t[:, :].rearrange("p (t d) -> p t d", t=TPB), x_own[:, :, :],
                                      ALU.add).then_inc(o_done, 1)

                def statistics(n):
                    dve.wait_ge(o_done, n + 1 + 1)
                    own_wait(dve, passed)
                    for t in range(TPB):
                        dve.bn_stats(stats[:, bass.ds(n * TPB + t, 1), :].rearrange("p t s -> p (t s)"),
                                     o_out[:, t, :]).then_inc(seen, 1)
                    dve.tensor_copy(first[:, bass.ds(n * TPB, TPB)], o_out[:, :, 0]).then_inc(seen, 1)

                def one(n, par, before):
                    for s in range(STEPS):
                        t, c = divmod(s, CPT)
                        bias(n, par, s)
                        if before and s < OUT:
                            lows(n - 1, s)
                        if c == CPT - 1:
                            maximum(n, t)
                        if before == 2 and s == START + 1:
                            add_input(n - 2)
                        if before == 2 and s == START + 3:
                            statistics(n - 2)
                        if before and s == START + 2:
                            denominators(n - 1, 1 - par)

                def tail(n, par):
                    add_input(n - 1)
                    statistics(n - 1)
                    dve.wait_ge(seen, n * (TPB + 1))
                    for s in range(OUT):
                        lows(n, s)
                        if START <= s < START + NB - 1:
                            for t in range(TPB):
                                merge_heads(dve, stats, mv, (s - START) * TPB + t, merged)
                        if s == START + 2:
                            denominators(n, par)
                    add_input(n)
                    statistics(n)

                all_blocks(dve, one, tail)


def bin_experts(nc, sem, h1_dram, stats, first, mv, w_bins, steps_in, tri_in, ident, out):
    RING = 4
    assert TILES % RING == 0
    EARLY = 2

    with ExitStack() as ctx:
        def sb(name, shape, dt=F32):
            return ctx.enter_context(nc.sbuf_tensor(name, shape, dt))

        w_hi = sb("f_w_hi", [P, BINS, CC, C], F32R)
        w_rest = sb("f_w_rest", [P, BINS, CC, C])
        widths = [BINS - 1, JT, TILES, P, JT]
        steps = sb("f_steps", [P, sum(widths)])
        thresholds, full_tiles, tile_numbers, lane_numbers, numbers = [
            steps[:, sum(widths[:i]):sum(widths[:i + 1])] for i in range(len(widths))]
        eps = sb("f_eps", [P, 1])
        warm = sb("f_warm", [P, 1])
        tri_raw = sb("f_tri_raw", [P, 2 * P])
        tri = sb("f_tri", [P, 2 * P], F32R)

        dev = sb("f_dev", [P, JT])
        root = sb("f_root", [P, JT])
        newton = sb("f_newton", [P, JT])
        norm = sb("f_norm", [P, JT, 2])
        y = sb("f_y", [P, JT])
        above = sb("f_above", [P, BINS + 1, JT])
        in_bin = sb("f_in_bin", [P, BINS, JT], F32R)
        upto = [sb(f"f_upto{i}", [P, BINS, 2 * JT]) for i in range(2)]
        filled = sb("f_filled", [P, BINS, JT])
        ends = [sb(f"f_ends{i}", [P, 2 * BINS]) for i in range(2)]
        starts = sb("f_starts", [P, BINS])
        place = sb("f_place", [P, BINS, JT])
        slot_f = sb("f_slot_f", [P, JT])
        slot = sb("f_slot", [P, JT], I32)
        lane = sb("f_lane", [P, JT], I32)
        tile_of = sb("f_tile_of", [P, JT], I32)
        passed_ends = sb("f_passed_ends", [P, TILES, BINS - 1])
        tile_bin_f = sb("f_tile_bin_f", [P, TILES])
        tile_bin = sb("f_tile_bin", [P, TILES], I32)
        lane_f = sb("f_lane_f", [P, JT])
        tile_f = sb("f_tile_f", [P, JT])
        in_lane = sb("f_in_lane", [P, JT, P], F32R)
        in_tile = sb("f_in_tile", [P, JT, TILES])
        number_in_tile = sb("f_number_in_tile", [P, JT, TILES], F32R)
        from_all = sb("f_from_all", [P, TILES])
        to_all = sb("f_to_all", [P, TILES])
        from_row = [sb(f"f_from{i}", [P, 1], I32) for i in range(RING)]
        to_row = [sb(f"f_to{i}", [P, 1], I32) for i in range(RING)]
        h1 = [sb(f"f_h1{i}", [P, C + 2]) for i in range(RING)]
        res = [sb(f"f_res{i}", [P, C]) for i in range(RING)]
        xf = [sb(f"f_xf{i}", [P, C]) for i in range(2)]
        xf_hi = [sb(f"f_xfhi{i}", [P, CC, P], F32R) for i in range(2)]
        xf_lo = [sb(f"f_xflo{i}", [P, CC, P], F32R) for i in range(2)]

        count_ps = ctx.enter_context(nc.psum_tensor("f_count", [P, 2, BINS * JT], F32))
        slot_ps = ctx.enter_context(nc.psum_tensor("f_slot_ps", [P, TILES], F32))
        bank = [ctx.enter_context(nc.psum_tensor(f"f_bank{i}", [P, C], F32)) for i in range(2)]
        turn_ps = [ctx.enter_context(nc.psum_tensor(f"f_turn{i}", [P, C], F32)) for i in range(2)]

        passed = sem("f_passed")
        const_loaded = sem("f_const_loaded")
        set_done = sem("f_set_done")
        tri_done = sem("f_tri_done")
        w_loaded = [sem(f"f_w_loaded{k}") for k in range(BINS)]
        w_hi_done = sem("f_w_hi_done")
        w_lo_done = sem("f_w_lo_done")
        last_w_done = sem("f_last_w_done")
        norm_stored = sem("f_norm_stored")
        stats_done = sem("f_stats_done")
        dev_done = sem("f_dev_done")
        route_step = sem("f_route_step")
        counted = sem("f_counted")
        bins_done = sem("f_bins_done")
        lanes_done = sem("f_lanes_done")
        numbered = sem("f_numbered")
        slots_filled = sem("f_slots_filled")
        slots_done = sem("f_slots_done")
        from_done = sem("f_from_done")
        gathered = [sem(f"f_gathered{i}") for i in range(RING)]
        xf_done = sem("f_xf_done")
        turned = sem("f_turned")
        hi_done = sem("f_hi_done")
        lo_done = sem("f_lo_done")
        product_done = sem("f_product_done")
        res_done = sem("f_res_done")
        scattered = [sem(f"f_scattered{i}") for i in range(RING)]

        def low_w(eng, k, done):
            eng.wait_ge(w_hi_done, k + 1)
            eng.tensor_tensor(w_rest[:, k, :, :].bitcast(F32R), w_rest[:, k, :, :], f32(w_hi[:, k, :, :]), ALU.subtract) \
               .then_inc(done, 1)

        def all_tiles(eng, one):
            for j in range(2 * RING):
                one(j, j % RING)
            with eng.Fori(2, TILES // RING - 1) as m:
                for i in range(RING):
                    one(m * RING + i, i, True, True)
            for i in range(RING):
                one(TILES - RING + i, i)

        with nc.Block() as block:

            @block.sync
            def _(sp):
                sp.dma_start(steps[:, :], steps_in).then_inc(const_loaded, 16)
                sp.dma_start(tri_raw[:, :], tri_in).then_inc(const_loaded, 16)
                for k in range(BINS):
                    sp.dma_start(w_rest[:, k, :, :], w_bins[k].rearrange("(c p) n -> p c n", p=P)) \
                      .then_inc(w_loaded[k], 16)
                    if k == EARLY:
                        sp.wait_ge(route_step, NORMED)
                        sp.dma_start(h1_dram[:, C:].rearrange("(t p) c -> p t c", p=P), norm[:, :, :]) \
                          .then_inc(norm_stored, 16)

            @block.gpsimd
            def _(pool):
                for i in range(2):
                    pool.memset(upto[i][:, :, 0:JT], 0.0).then_inc(set_done, 1)
                    pool.memset(ends[i][:, 0:BINS], 0.0).then_inc(set_done, 1)
                pool.memset(eps[:, :], EPS_T).then_inc(set_done, 1)
                pool.memset(above[:, 0, :], 1.0).then_inc(set_done, 1)
                pool.memset(above[:, BINS, :], 0.0).then_inc(set_done, 1)
                for k in range(EARLY):
                    low_w(pool, k, w_lo_done)
                pool.wait_ge(route_step, PLACED + 1)
                pool.tensor_tensor(number_in_tile[:, :, :], in_tile[:, :, :],
                                   numbers.unsqueeze(2).to_broadcast([P, JT, TILES]), ALU.mult).then_inc(numbered, 1)
                pool.wait_ge(norm_stored, 16)

                def gather(j, i):
                    pool.wait_ge(from_done, j + 1)
                    own_wait(pool, passed)
                    pool.indirect_dma_start(h1[i][:, :], None, h1_dram, bass.IndirectOffsetOnAxis(from_row[i][:, :], 0)) \
                        .then_inc(gathered[i], 16)

                def scatter(j, i):
                    pool.indirect_dma_start(out, bass.IndirectOffsetOnAxis(to_row[i][:, :], 0), res[i][:, :], None,
                                            bounds_check=T - 1, oob_is_err=False).then_inc(scattered[i], 16)

                def one(j, i, before=False, after=False):
                    if before or j >= 1:
                        pool.wait_ge(res_done, j)
                        own_wait(pool, passed)
                    if after or j + RING - 1 < TILES:
                        gather(j + RING - 1, (i - 1) % RING)
                    if before or j >= 1:
                        scatter(j - 1, (i - 1) % RING)

                for j in range(RING - 1):
                    gather(j, j)
                low_w(pool, BINS - 1, last_w_done)
                all_tiles(pool, one)
                pool.wait_ge(res_done, TILES)
                scatter(TILES - 1, RING - 1)
                for i in range(RING):
                    pool.wait_ge(scattered[i], 16 * (TILES // RING))

            @block.tensor
            def _(pe):
                def turn(j, i):
                    pe.wait_ge(xf_done, j + 1)
                    for c in range(CC):
                        mm = pe.transpose(turn_ps[i % 2][:, c * P:(c + 1) * P], xf[i % 2][:, c * P:(c + 1) * P],
                                          ident[:, :])
                    mm.then_inc(turned, 1)

                def one(j, i, before=False, after=False):
                    if after or j + 1 < TILES:
                        turn(j + 1, i + 1)
                    bin_no = pe.value_load(tile_bin[0:1, bass.ds(j, 1)], min_val=0, max_val=BINS - 1)
                    pe.wait_ge(w_lo_done, bin_no + 1)
                    pe.wait_ge(lo_done, j + 1)
                    if before or j >= 2:
                        pe.wait_ge(res_done, j - 1)
                    for c in range(CC):
                        hi = w_hi[:, bass.ds(bin_no, 1), c, :].rearrange("p k n -> p (k n)")
                        lo = w_rest[:, bass.ds(bin_no, 1), c, :].rearrange("p k n -> p (k n)").bitcast(F32R)
                        mm = split_product(pe, bank[i % 2][:, :], xf_hi[i % 2][:, c, :], xf_lo[i % 2][:, c, :],
                                           hi, lo, c == 0, c == CC - 1)
                    mm.then_inc(product_done, 1)

                pe.wait_ge(tri_done, 1)
                pe.wait_ge(bins_done, 1)
                for i in range(2):
                    pe.matmul(count_ps[:, i, :], tri[:, i * P:(i + 1) * P],
                              in_bin[:, :, :].rearrange("p k t -> p (k t)"), start=True, stop=True).then_inc(counted, 1)
                pe.wait_ge(lanes_done, 1)
                pe.wait_ge(numbered, 1)
                for t in range(JT):
                    mm = pe.matmul(slot_ps[:, :], in_lane[:, t, :], number_in_tile[:, t, :], start=t == 0, stop=t == JT - 1)
                mm.then_inc(slots_filled, 1)
                pe.wait_ge(route_step, ROUTED)
                turn(0, 0)
                all_tiles(pe, one)

            @block.scalar
            def _(act):
                def high(j, i, before=False, after=False):
                    act.wait_ge(turned, j + 1)
                    if before or j >= 2:
                        act.wait_ge(product_done, j - 1)
                    act.activation(xf_hi[i % 2][:, :, :], turn_ps[i % 2][:, :].rearrange("p (c t) -> p c t", c=CC),
                                   ACT.Copy).then_inc(hi_done, 1)

                act.wait_ge(set_done, 7)
                act.activation(warm[:, :], eps[:, :], ACT.Sqrt)
                act.wait_ge(stats_done, TPB)
                act.activation(dev[:, :], mv[:, :, 1], ACT.Sqrt, bias=eps[:, 0:1]).then_inc(dev_done, 1)
                act.wait_ge(const_loaded, 32)
                act.activation(tri[:, :], tri_raw[:, :], ACT.Copy).then_inc(tri_done, 1)
                for k in range(BINS):
                    act.wait_ge(w_loaded[k], 16)
                    act.activation(w_hi[:, k, :, :], w_rest[:, k, :, :], ACT.Copy).then_inc(w_hi_done, 1)
                all_tiles(act, high)

            @block.vector
            def _(dve):
                for t in range(JT - TPB, JT):
                    merge_heads(dve, stats, mv, t, stats_done)
                dve.wait_ge(dev_done, 1)
                dve.reciprocal(root[:, :], dev[:, :]).then_inc(route_step, 1)
                dve.wait_ge(route_step, 1)
                dve.tensor_tensor(newton[:, :], root[:, :], root[:, :], ALU.mult).then_inc(route_step, 1)
                dve.wait_ge(route_step, 2)
                dve.scalar_tensor_tensor(out=newton[:, :], in0=mv[:, :, 1], scalar=EPS_T, in1=newton[:, :],
                                         op0=ALU.add, op1=ALU.mult).then_inc(route_step, 1)
                dve.wait_ge(route_step, 3)
                dve.tensor_scalar(newton[:, :], newton[:, :], -0.5, 1.5, ALU.mult, ALU.add).then_inc(route_step, 1)
                dve.wait_ge(route_step, 4)
                dve.tensor_tensor(norm[:, :, 1], root[:, :], newton[:, :], ALU.mult).then_inc(route_step, 1)
                dve.tensor_copy(norm[:, :, 0], mv[:, :, 0]).then_inc(route_step, 1)
                dve.tensor_tensor(y[:, :], first[:, 0:JT], mv[:, :, 0], ALU.subtract).then_inc(route_step, 1)
                dve.wait_ge(route_step, 7)
                dve.tensor_tensor(y[:, :], y[:, :], norm[:, :, 1], ALU.mult).then_inc(route_step, 1)
                dve.wait_ge(route_step, 8)
                dve.wait_ge(set_done, 7)
                dve.wait_ge(const_loaded, 32)
                dve.tensor_tensor(above[:, 1:BINS, :], y[:, :].unsqueeze(1).to_broadcast([P, BINS - 1, JT]),
                                  thresholds.unsqueeze(2).to_broadcast([P, BINS - 1, JT]), ALU.is_gt) \
                   .then_inc(route_step, 1)
                dve.wait_ge(route_step, 9)
                dve.tensor_tensor(in_bin[:, :, :], above[:, 0:BINS, :], above[:, 1:BINS + 1, :], ALU.subtract) \
                   .then_inc(bins_done, 1)
                dve.wait_ge(counted, 2)
                dve.tensor_copy(upto[0][:, :, JT:], count_ps[:, 1, :].rearrange("p (k t) -> p k t", k=BINS)) \
                   .then_inc(route_step, 1)
                for i in range(5):
                    dve.wait_ge(route_step, 10 + i)
                    dve.tensor_tensor(upto[(i + 1) % 2][:, :, JT:], upto[i % 2][:, :, JT:],
                                      upto[i % 2][:, :, JT - (1 << i):2 * JT - (1 << i)], ALU.add) \
                       .then_inc(route_step, 1)
                sums = upto[1]
                dve.wait_ge(route_step, 15)
                dve.tensor_tensor(filled[:, :, :], sums[:, :, 2 * JT - 1:].to_broadcast([P, BINS, JT]),
                                  full_tiles.unsqueeze(1).to_broadcast([P, BINS, JT]), ALU.is_gt) \
                   .then_inc(route_step, 1)
                dve.wait_ge(route_step, 16)
                dve.tensor_reduce(ends[0][:, BINS:], filled[:, :, :], AX.X, ALU.add).then_inc(route_step, 1)
                for i in range(3):
                    dve.wait_ge(route_step, 17 + i)
                    dve.tensor_tensor(ends[(i + 1) % 2][:, BINS:], ends[i % 2][:, BINS:],
                                      ends[i % 2][:, BINS - (1 << i):2 * BINS - (1 << i)], ALU.add) \
                       .then_inc(route_step, 1)
                dve.wait_ge(route_step, 20)
                dve.tensor_scalar(starts[:, :], ends[1][:, BINS - 1:2 * BINS - 1], float(P), None, ALU.mult) \
                   .then_inc(route_step, 1)
                dve.tensor_tensor(place[:, :, :], count_ps[:, 0, :].rearrange("p (k t) -> p k t", k=BINS),
                                  sums[:, :, JT - 1:2 * JT - 1], ALU.add).then_inc(route_step, 1)
                dve.wait_ge(route_step, 22)
                dve.tensor_tensor(place[:, :, :], place[:, :, :], starts[:, :].unsqueeze(2).to_broadcast([P, BINS, JT]),
                                  ALU.add).then_inc(route_step, 1)
                dve.wait_ge(route_step, 23)
                dve.tensor_tensor(place[:, :, :], place[:, :, :], f32(in_bin[:, :, :]), ALU.mult).then_inc(route_step, 1)
                dve.wait_ge(route_step, 24)
                dve.tensor_reduce(slot_f[:, :], place[:, :, :].rearrange("p k t -> p t k"), AX.X, ALU.add) \
                   .then_inc(route_step, 1)
                dve.wait_ge(route_step, 25)
                dve.tensor_copy(slot[:, :], slot_f[:, :]).then_inc(route_step, 1)
                dve.wait_ge(route_step, 26)
                dve.tensor_scalar(lane[:, :], slot[:, :], P - 1, None, ALU.bitwise_and).then_inc(route_step, 1)
                dve.tensor_scalar(tile_of[:, :], slot[:, :], LOG_P, None, ALU.logical_shift_right).then_inc(route_step, 1)
                dve.wait_ge(route_step, 28)
                dve.tensor_copy(lane_f[:, :], lane[:, :]).then_inc(route_step, 1)
                dve.tensor_copy(tile_f[:, :], tile_of[:, :]).then_inc(route_step, 1)
                dve.wait_ge(route_step, PLACED)
                dve.tensor_tensor(in_tile[:, :, :], tile_f[:, :].unsqueeze(2).to_broadcast([P, JT, TILES]),
                                  tile_numbers.unsqueeze(1).to_broadcast([P, JT, TILES]), ALU.is_equal) \
                   .then_inc(route_step, 1)
                dve.tensor_tensor(in_lane[:, :, :], lane_f[:, :].unsqueeze(2).to_broadcast([P, JT, P]),
                                  lane_numbers.unsqueeze(1).to_broadcast([P, JT, P]), ALU.is_equal) \
                   .then_inc(lanes_done, 1)
                dve.tensor_tensor(passed_ends[:, :, :],
                                  tile_numbers.unsqueeze(2).to_broadcast([P, TILES, BINS - 1]),
                                  ends[1][:, BINS:2 * BINS - 1].unsqueeze(1).to_broadcast([P, TILES, BINS - 1]),
                                  ALU.is_ge).then_inc(route_step, 1)
                dve.wait_ge(route_step, 32)
                dve.tensor_reduce(tile_bin_f[:, :], passed_ends[:, :, :], AX.X, ALU.add).then_inc(route_step, 1)
                dve.wait_ge(route_step, 33)
                dve.tensor_copy(tile_bin[:, :], tile_bin_f[:, :]).then_inc(route_step, 1)
                dve.wait_ge(w_lo_done, EARLY)
                low_w(dve, EARLY, w_lo_done)
                low_w(dve, EARLY + 1, w_lo_done)
                dve.wait_ge(slots_filled, 1)
                dve.tensor_scalar(to_all[:, :], slot_ps[:, :], float(T), None, ALU.add).then_inc(slots_done, 1)
                dve.tensor_scalar(from_all[:, :], slot_ps[:, :], float(T), T - 1.0, ALU.add, ALU.min).then_inc(slots_done, 1)

                def gather_rows(j, i):
                    dve.tensor_copy(from_row[i][:, :], from_all[:, bass.ds(j, 1)]) \
                       .then_inc(from_done, 1)

                def normalise(j, i):
                    dve.wait_ge(gathered[i], 16 * (j // RING + 1))
                    own_wait(dve, passed)
                    dve.tensor_scalar(xf[i % 2][:, :], h1[i][:, 0:C], h1[i][:, C:C + 1], h1[i][:, C + 1:C + 2],
                                      ALU.subtract, ALU.mult).then_inc(xf_done, 1)

                def low(j, i):
                    dve.wait_ge(hi_done, j + 1)
                    dve.tensor_tensor(xf_lo[i % 2][:, :, :], turn_ps[i % 2][:, :].rearrange("p (c t) -> p c t", c=CC),
                                      f32(xf_hi[i % 2][:, :, :]), ALU.subtract).then_inc(lo_done, 1)

                def result(j, i, before):
                    if before or j >= RING:
                        dve.wait_ge(scattered[i], 16 * (j // RING))
                        own_wait(dve, passed)
                    dve.tensor_copy(to_row[i][:, :], to_all[:, bass.ds(j, 1)])
                    dve.wait_ge(product_done, j + 1)
                    own_wait(dve, passed)
                    dve.tensor_tensor(res[i][:, :], bank[i % 2][:, :], h1[i][:, 0:C], ALU.add).then_inc(res_done, 1)

                def one(j, i, before=False, after=False):
                    if after or j + RING - 1 < TILES:
                        gather_rows(j + RING - 1, (i - 1) % RING)
                    if before or j >= 1:
                        result(j - 1, (i - 1) % RING, before)
                    if after or j + 1 < TILES:
                        low(j + 1, (i + 1) % RING)
                    if after or j + 2 < TILES:
                        normalise(j + 2, (i + 2) % RING)
                    if not before and j == 0:
                        for k in range(EARLY + 2, BINS - 1):
                            low_w(dve, k, w_lo_done)
                        dve.wait_ge(last_w_done, 1)
                        dve.sem_inc(w_lo_done, 1)

                dve.wait_ge(slots_done, 2)
                for j in range(RING - 1):
                    gather_rows(j, j)
                normalise(0, 0)
                normalise(1, 1)
                low(0, 0)
                all_tiles(dve, one)
                result(TILES - 1, RING - 1, True)


def metaformer_block(nc, x_t, w_qkv_t, rel_t, w_bins, ident_in, steps, tri, out):
    def dram(name, shape):
        return nc.dram_tensor(name, shape, F32, kind="Internal").ap()

    q_dram = dram("q_halves", [HEADS, P, 2, T])
    k_dram = dram("k_halves", [HEADS, P, 2, T])
    v_dram = dram("v_halves", [HEADS, P, 2, JT * DH])
    rel_dram = dram("rel_products", [HEADS, T, REL])
    h1_dram = dram("h1", [T, C + 2])

    with ExitStack() as ctx:
        def sem(name):
            return ctx.enter_context(nc.semaphore(name))

        ident = ctx.enter_context(nc.sbuf_tensor("identity", [P, P], F32))
        stats = ctx.enter_context(nc.sbuf_tensor("h1_stats", [P, HEADS * JT, 6], F32))
        first = ctx.enter_context(nc.sbuf_tensor("h1_first", [P, HEADS * JT], F32))
        mv = ctx.enter_context(nc.sbuf_tensor("h1_mv", [P, JT, 2], F32))
        with ExitStack() as pre:
            k_sb = pre.enter_context(nc.sbuf_tensor("k", [P, 2, T], F32R))
            q_sb = pre.enter_context(nc.sbuf_tensor("q", [P, 2, B], F32R))
            lw = pre.enter_context(nc.sbuf_tensor("bias_by_column", [P, TPB, SIDE], F32))
            lh = pre.enter_context(nc.sbuf_tensor("bias_by_row", [P, TPB, SIDE], F32))
            k_loaded = [sem(f"k_loaded{i}") for i in range(CPT)]
            q_loaded = [sem(f"q_loaded{i}") for i in range(TPB)]
            bias_loaded = sem("bias_loaded")
            ahead = (k_sb, q_sb, lw, lh, k_loaded, q_loaded, bias_loaded)
            project(nc, sem, x_t, w_qkv_t, rel_t, ident_in, ident, q_dram, k_dram, v_dram, rel_dram, *ahead)
            attend(nc, sem, q_dram, k_dram, v_dram, rel_dram, x_t, h1_dram, stats, first, mv, ident, *ahead)
        bin_experts(nc, sem, h1_dram, stats, first, mv, w_bins, steps, tri, ident, out)


def kernel(x, L0_conv_w_qkv, L0_conv_rel_height, L0_conv_rel_width, L0_ffn_W):
    import numpy as np
    import concourse.bacc as bacc
    from concourse.bass_utils import run_bass_kernel_spmd

    x = np.asarray(x).reshape(C, T)
    rel = np.zeros((P, REL), np.float32)
    rel[:, :2 * SIDE - 1] = np.asarray(L0_conv_rel_width).T
    rel[:, P:P + 2 * SIDE - 1] = np.asarray(L0_conv_rel_height).T
    steps = np.tile(np.concatenate([THRESHOLDS, np.arange(JT) * P, np.arange(TILES), np.arange(P)]), (P, 1))
    steps = np.concatenate([steps, np.arange(T).reshape(JT, P).T - T], axis=1).astype(np.float32)
    arrays = {
        "x_t": np.ascontiguousarray(x.T),
        "w_qkv_t": np.ascontiguousarray(np.asarray(L0_conv_w_qkv).T),
        "rel_t": rel,
        "w_bins": np.ascontiguousarray(np.asarray(L0_ffn_W)),
        "ident": np.eye(P, dtype=np.float32),
        "steps": steps,
        "tri": np.concatenate([np.triu(np.ones((P, P), np.float32), 1), np.ones((P, P), np.float32)], axis=1),
    }
    nc = bacc.Bacc("TRN2", target_bir_lowering=False, num_devices=1)
    ins = [nc.dram_tensor(name, a.shape, F32, kind="ExternalInput").ap() for name, a in arrays.items()]
    out = nc.dram_tensor("out", (T, C), F32, kind="ExternalOutput").ap()
    metaformer_block(nc, *ins, out)
    result = run_bass_kernel_spmd(nc, [arrays], core_ids=[0]).results[0]["out"]
    return np.ascontiguousarray(result.T).reshape(1, C, SIDE, SIDE)
```
